# Optimizing a Trainium2 kernel written in Bass

```python
import numpy as np
import jax
import jax.numpy as jnp

def _softmax(x, axis=-1):
    return jax.nn.softmax(x, axis=axis)

def _gelu(x):
    return jax.nn.gelu(x, approximate=True)

def _silu(x):
    return jax.nn.silu(x)

def _sigmoid(x):
    return jax.nn.sigmoid(x)

def _layernorm(x, axis=-1, eps=1e-05):
    m = jnp.mean(x, axis=axis, keepdims=True)
    v = jnp.var(x, axis=axis, keepdims=True)
    return (x - m) / jnp.sqrt(v + eps)

def _scatter_add(tgt, idx, src, axis=0):
    return tgt.at[idx].add(src)

def _segment_sum(src, seg, n):
    return jax.ops.segment_sum(src, seg, n)
kernel_name = 'mk_seq_postln_d2_jaxref_r8_b3aab1'

def setup_inputs(seed: int=0):
    np.random.seed(seed)
    _w = jnp.asarray

    def _L0_attn_setup():
        import jax, jax.numpy as jnp
        import numpy as np
        D_MODEL = 128

        def _reference_tuple_inner(x, W_state, b_state, W_gate, b_gate):
            B, T, C = x.shape
            px = jnp.einsum('btc,dc->btd', x, W_state) + b_state
            g = jax.nn.sigmoid(jnp.einsum('btc,dc->btd', x, W_gate) + b_gate)

            def step(state, inp):
                p_t, g_t = inp
                state = jnp.tanh(p_t + state)
                return (state, g_t * state)
            s0 = jnp.zeros((B, C), dtype=x.dtype)
            final_state, outs = jax.lax.scan(step, s0, (px.transpose(1, 0, 2), g.transpose(1, 0, 2)))
            return (outs.transpose(1, 0, 2), final_state)
        key = jax.random.key(seed)
        k1, k2, k3, k4, k5 = jax.random.split(key, 5)
        B, T, C = (8, 512, D_MODEL)
        bound = 1.0 / np.sqrt(C)
        return {'x': jax.random.normal(k1, (B, T, C), dtype=jnp.float32), 'W_state': jax.random.uniform(k2, (C, C), dtype=jnp.float32, minval=-bound, maxval=bound), 'b_state': jax.random.uniform(k3, (C,), dtype=jnp.float32, minval=-bound, maxval=bound), 'W_gate': jax.random.uniform(k4, (C, C), dtype=jnp.float32, minval=-bound, maxval=bound), 'b_gate': jax.random.uniform(k5, (C,), dtype=jnp.float32, minval=-bound, maxval=bound)}
    _L0_attn_in = _L0_attn_setup()

    def _L0_ffn_setup():
        import jax, jax.numpy as jnp
        import numpy as np
        B, S, H, F, E = (1, 256, 128, 256, 8)

        def _swiglu(x, wg, wu, wd):
            return jax.nn.silu(x @ wg.T) * (x @ wu.T) @ wd.T
        key = jax.random.key(seed)
        ks = jax.random.split(key, 8)
        sc = 1.0 / np.sqrt(H)
        scf = 1.0 / np.sqrt(F)
        return {'hidden_states': jax.random.normal(ks[0], (B, S, H), jnp.float32), 'gate_w': jax.random.normal(ks[1], (E, H), jnp.float32) * sc, 'shared_gate': jax.random.normal(ks[2], (F, H), jnp.float32) * sc, 'shared_up': jax.random.normal(ks[3], (F, H), jnp.float32) * sc, 'shared_down': jax.random.normal(ks[4], (H, F), jnp.float32) * scf, 'r_gate': jax.random.normal(ks[5], (E, F, H), jnp.float32) * sc, 'r_up': jax.random.normal(ks[6], (E, F, H), jnp.float32) * sc, 'r_down': jax.random.normal(ks[7], (E, H, F), jnp.float32) * scf}
    _L0_ffn_in = _L0_ffn_setup()

    def _L1_attn_setup():
        import jax, jax.numpy as jnp
        import numpy as np
        D_MODEL = 128
        NHEAD = 16

        def unitnorm(v):
            n = jnp.sqrt(jnp.sum(v * v, axis=-1, keepdims=True))
            return v / jnp.maximum(n, 1e-12)

        def _reference_tuple_inner(inp, Wq_w, Wq_b, Wk_w, Wk_b, Wv_w, Wv_b, Wo_w, Wo_b, Ww_w, Ww_b, Wr_w, Wr_b):
            src = inp
            S, B, d = inp.shape
            n = NHEAD
            k = (src @ Wk_w.T + Wk_b).reshape(S, B, n, -1)
            v = (src @ Wv_w.T + Wv_b).reshape(S, B, n, -1)
            q = (inp @ Wq_w.T + Wq_b).reshape(S, B, n, -1)
            k = unitnorm(k)
            q = unitnorm(q)
            w = jax.nn.sigmoid(src @ Ww_w.T + Ww_b)
            A = jnp.einsum('sbnq,sbnv->bnvq', k, v * w[:, :, :, None])
            r = jax.nn.sigmoid(inp @ Wr_w.T + Wr_b)
            out = jnp.einsum('sbnq,bnvq->sbnv', q, A) * r[:, :, :, None]
            out = out.reshape(S, B, d)
            out = out @ Wo_w.T + Wo_b
            return (out, A)
        key = jax.random.key(seed)
        ks = jax.random.split(key, 14)
        d = D_MODEL
        sc = 1.0 / np.sqrt(d)
        inp = jax.random.normal(ks[0], (256, 8, d), dtype=jnp.float32)

        def lin(kw, kb, out_dim):
            W = jax.random.uniform(kw, (out_dim, d), minval=-sc, maxval=sc, dtype=jnp.float32)
            b = jax.random.uniform(kb, (out_dim,), minval=-sc, maxval=sc, dtype=jnp.float32)
            return (W, b)
        Wq_w, Wq_b = lin(ks[1], ks[2], d)
        Wk_w, Wk_b = lin(ks[3], ks[4], d)
        Wv_w, Wv_b = lin(ks[5], ks[6], d)
        Wo_w, Wo_b = lin(ks[7], ks[8], d)
        Ww_w, Ww_b = lin(ks[9], ks[10], NHEAD)
        Wr_w, Wr_b = lin(ks[11], ks[12], NHEAD)
        return {'inp': inp, 'Wq_w': Wq_w, 'Wq_b': Wq_b, 'Wk_w': Wk_w, 'Wk_b': Wk_b, 'Wv_w': Wv_w, 'Wv_b': Wv_b, 'Wo_w': Wo_w, 'Wo_b': Wo_b, 'Ww_w': Ww_w, 'Ww_b': Ww_b, 'Wr_w': Wr_w, 'Wr_b': Wr_b}
    _L1_attn_in = _L1_attn_setup()

    def _L1_ffn_setup():
        import jax, jax.numpy as jnp
        import numpy as np
        DIM = 128
        DEPTH = 6
        HEADS = 16
        DIM_HEAD = 64
        WINDOW = 32
        INNER = HEADS * DIM_HEAD
        DIM_INNER = int(DIM * 4 * 2 / 3)
        QK_SCALE = 8.0

        def shift_tokens(t):
            a, s = jnp.split(t, 2, -1)
            s = jnp.pad(s, ((0, 0), (1, 0), (0, 0)))[:, :-1]
            return jnp.concatenate([a, s], -1)

        def l2norm(t):
            return t / jnp.maximum(jnp.linalg.norm(t, axis=-1, keepdims=True), 1e-12)

        def rotate_half(x):
            x1, x2 = jnp.split(x, 2, -1)
            return jnp.concatenate([-x2, x1], -1)

        def rotary_tables(n):
            half = jnp.arange(0, DIM_HEAD, 2, dtype=jnp.float32)
            inv_freq = 1.0 / 10000.0 ** (half / DIM_HEAD)
            t = jnp.arange(n, dtype=jnp.float32)
            freqs = t[:, None] * inv_freq[None, :]
            freqs = jnp.concatenate([freqs, freqs], -1)
            base_scale = (half + 0.4 * DIM_HEAD) / (1.4 * DIM_HEAD)
            power = (t - n // 2) / (WINDOW // 2)
            scale = base_scale[None, :] ** power[:, None]
            scale = jnp.concatenate([scale, scale], -1)
            return (freqs, scale)

        def local_attention(q, k, v):
            b, h, n, d = q.shape
            w = WINDOW
            nw = n // w
            bq = q.reshape(b, h, nw, w, d)
            bk = k.reshape(b, h, nw, w, d)
            bv = v.reshape(b, h, nw, w, d)

            def look(t):
                p = jnp.pad(t, ((0, 0), (0, 0), (1, 0), (0, 0), (0, 0)))
                return jnp.concatenate([p[:, :, :nw], p[:, :, 1:]], axis=3)
            bk2, bv2 = (look(bk), look(bv))
            seq = jnp.arange(n).reshape(nw, w)
            seq_p = jnp.pad(seq, ((1, 0), (0, 0)), constant_values=-1)
            jt = jnp.concatenate([seq_p[:nw], seq_p[1:]], axis=1)
            it = seq[:, :, None]
            jb = jt[:, None, :]
            mask = (it < jb) | (it > jb + w) | (jb == -1)
            sim = jnp.einsum('bhwie,bhwje->bhwij', bq, bk2) * QK_SCALE
            sim = jnp.where(mask, -jnp.finfo(sim.dtype).max, sim)
            attn = jax.nn.softmax(sim, -1)
            out = jnp.einsum('bhwij,bhwje->bhwie', attn, bv2)
            return out.reshape(b, h, n, d)

        def attn_layer(x, Wqkv, qs, ksc, Wo):
            b, n, _ = x.shape
            qkv = x @ Wqkv
            q, k, v = jnp.split(qkv, 3, -1)
            sh = lambda t: t.reshape(b, n, HEADS, DIM_HEAD).transpose(0, 2, 1, 3)
            q, k, v = (sh(q), sh(k), sh(v))
            q = l2norm(q) * qs
            k = l2norm(k) * ksc
            freqs, scale = rotary_tables(n)
            cos, sin = (jnp.cos(freqs), jnp.sin(freqs))
            q = q * cos * scale + rotate_half(q) * sin * scale
            inv = 1.0 / scale
            k = k * cos * inv + rotate_half(k) * sin * inv
            out = local_attention(q, k, v)
            out = out.transpose(0, 2, 1, 3).reshape(b, n, INNER)
            return out @ Wo

        def ffn_layer(x, g, bln, W1, b1, W2, b2):
            mu = x.mean(-1, keepdims=True)
            var = ((x - mu) ** 2).mean(-1, keepdims=True)
            xn = (x - mu) / jnp.sqrt(var + 1e-05) * g + bln
            hg = xn @ W1 + b1
            a, gate = jnp.split(hg, 2, -1)
            return a * jax.nn.gelu(gate, approximate=False) @ W2 + b2
        key = jax.random.key(seed)
        ks = jax.random.split(key, 8)
        B, N = (2, 256)
        init = lambda k, shape: jax.random.normal(k, shape, jnp.float32) * 0.02
        return {'x': jax.random.normal(ks[0], (B, N, DIM), jnp.float32), 'Wqkv': init(ks[1], (DEPTH, DIM, 3 * INNER)), 'q_scale': jnp.ones((DEPTH, DIM_HEAD), jnp.float32), 'k_scale': jnp.ones((DEPTH, DIM_HEAD), jnp.float32), 'Wo': init(ks[2], (DEPTH, INNER, DIM)), 'ln_g': jnp.ones((DEPTH, DIM), jnp.float32), 'ln_b': jnp.zeros((DEPTH, DIM), jnp.float32), 'W1': init(ks[3], (DEPTH, DIM, 2 * DIM_INNER)), 'b1': jnp.zeros((DEPTH, 2 * DIM_INNER), jnp.float32), 'W2': init(ks[4], (DEPTH, DIM_INNER, DIM)), 'b2': jnp.zeros((DEPTH, DIM), jnp.float32)}
    _L1_ffn_in = _L1_ffn_setup()
    _d = {'L0_attn_x': _L0_attn_in['x'], 'L0_attn_W_state': _L0_attn_in['W_state'], 'L0_attn_b_state': _L0_attn_in['b_state'], 'L0_attn_W_gate': _L0_attn_in['W_gate'], 'L0_attn_b_gate': _L0_attn_in['b_gate'], 'L0_ffn_gate_w': _L0_ffn_in['gate_w'], 'L0_ffn_shared_gate': _L0_ffn_in['shared_gate'], 'L0_ffn_shared_up': _L0_ffn_in['shared_up'], 'L0_ffn_shared_down': _L0_ffn_in['shared_down'], 'L0_ffn_r_gate': _L0_ffn_in['r_gate'], 'L0_ffn_r_up': _L0_ffn_in['r_up'], 'L0_ffn_r_down': _L0_ffn_in['r_down'], 'L1_attn_Wq_w': _L1_attn_in['Wq_w'], 'L1_attn_Wq_b': _L1_attn_in['Wq_b'], 'L1_attn_Wk_w': _L1_attn_in['Wk_w'], 'L1_attn_Wk_b': _L1_attn_in['Wk_b'], 'L1_attn_Wv_w': _L1_attn_in['Wv_w'], 'L1_attn_Wv_b': _L1_attn_in['Wv_b'], 'L1_attn_Wo_w': _L1_attn_in['Wo_w'], 'L1_attn_Wo_b': _L1_attn_in['Wo_b'], 'L1_attn_Ww_w': _L1_attn_in['Ww_w'], 'L1_attn_Ww_b': _L1_attn_in['Ww_b'], 'L1_attn_Wr_w': _L1_attn_in['Wr_w'], 'L1_attn_Wr_b': _L1_attn_in['Wr_b'], 'L1_ffn_Wqkv': _L1_ffn_in['Wqkv'], 'L1_ffn_q_scale': _L1_ffn_in['q_scale'], 'L1_ffn_k_scale': _L1_ffn_in['k_scale'], 'L1_ffn_Wo': _L1_ffn_in['Wo'], 'L1_ffn_ln_g': _L1_ffn_in['ln_g'], 'L1_ffn_ln_b': _L1_ffn_in['ln_b'], 'L1_ffn_W1': _L1_ffn_in['W1'], 'L1_ffn_b1': _L1_ffn_in['b1'], 'L1_ffn_W2': _L1_ffn_in['W2'], 'L1_ffn_b2': _L1_ffn_in['b2']}
    _x0 = _d['L0_attn_x']
    _d['L0_attn_x'] = jax.random.normal(jax.random.fold_in(jax.random.key(seed), 1), (16, 256, 128), dtype=_x0.dtype)
    del _x0
    return _d

def reference(L0_attn_x, L0_attn_W_state, L0_attn_b_state, L0_attn_W_gate, L0_attn_b_gate, L0_ffn_gate_w, L0_ffn_shared_gate, L0_ffn_shared_up, L0_ffn_shared_down, L0_ffn_r_gate, L0_ffn_r_up, L0_ffn_r_down, L1_attn_Wq_w, L1_attn_Wq_b, L1_attn_Wk_w, L1_attn_Wk_b, L1_attn_Wv_w, L1_attn_Wv_b, L1_attn_Wo_w, L1_attn_Wo_b, L1_attn_Ww_w, L1_attn_Ww_b, L1_attn_Wr_w, L1_attn_Wr_b, L1_ffn_Wqkv, L1_ffn_q_scale, L1_ffn_k_scale, L1_ffn_Wo, L1_ffn_ln_g, L1_ffn_ln_b, L1_ffn_W1, L1_ffn_b1, L1_ffn_W2, L1_ffn_b2):

    def _L0_attn_ref(x, W_state, b_state, W_gate, b_gate):
        import jax, jax.numpy as jnp
        import numpy as np
        D_MODEL = 128

        def _reference_tuple_inner(x, W_state, b_state, W_gate, b_gate):
            B, T, C = x.shape
            px = jnp.einsum('btc,dc->btd', x, W_state) + b_state
            g = jax.nn.sigmoid(jnp.einsum('btc,dc->btd', x, W_gate) + b_gate)

            def step(state, inp):
                p_t, g_t = inp
                state = jnp.tanh(p_t + state)
                return (state, g_t * state)
            s0 = jnp.zeros((B, C), dtype=x.dtype)
            final_state, outs = jax.lax.scan(step, s0, (px.transpose(1, 0, 2), g.transpose(1, 0, 2)))
            return (outs.transpose(1, 0, 2), final_state)
        return _reference_tuple_inner(x, W_state, b_state, W_gate, b_gate)[0]

    def _L0_ffn_ref(hidden_states, gate_w, shared_gate, shared_up, shared_down, r_gate, r_up, r_down):
        import jax, jax.numpy as jnp
        import numpy as np
        B, S, H, F, E = (1, 256, 128, 256, 8)

        def _swiglu(x, wg, wu, wd):
            return jax.nn.silu(x @ wg.T) * (x @ wu.T) @ wd.T
        b, s, h = hidden_states.shape
        x = hidden_states.reshape(-1, h)
        shared_out = _swiglu(x, shared_gate, shared_up, shared_down)
        logits = x @ gate_w.T
        top_id = jnp.argmax(logits, axis=-1)
        score = jax.nn.sigmoid(jnp.max(logits, axis=-1))
        xs = x * score[:, None]

        def body(acc, ws):
            wg, wu, wd, e = ws
            xe = jnp.where((top_id == e)[:, None], xs, 0.0)
            return (acc + _swiglu(xe, wg, wu, wd), None)
        acc0 = jnp.zeros_like(x)
        routed_out, _ = jax.lax.scan(body, acc0, (r_gate, r_up, r_down, jnp.arange(E)))
        return (shared_out + routed_out).reshape(b, s, h)

    def _L1_attn_ref(inp, Wq_w, Wq_b, Wk_w, Wk_b, Wv_w, Wv_b, Wo_w, Wo_b, Ww_w, Ww_b, Wr_w, Wr_b):
        import jax, jax.numpy as jnp
        import numpy as np
        D_MODEL = 128
        NHEAD = 16

        def unitnorm(v):
            n = jnp.sqrt(jnp.sum(v * v, axis=-1, keepdims=True))
            return v / jnp.maximum(n, 1e-12)

        def _reference_tuple_inner(inp, Wq_w, Wq_b, Wk_w, Wk_b, Wv_w, Wv_b, Wo_w, Wo_b, Ww_w, Ww_b, Wr_w, Wr_b):
            src = inp
            S, B, d = inp.shape
            n = NHEAD
            k = (src @ Wk_w.T + Wk_b).reshape(S, B, n, -1)
            v = (src @ Wv_w.T + Wv_b).reshape(S, B, n, -1)
            q = (inp @ Wq_w.T + Wq_b).reshape(S, B, n, -1)
            k = unitnorm(k)
            q = unitnorm(q)
            w = jax.nn.sigmoid(src @ Ww_w.T + Ww_b)
            A = jnp.einsum('sbnq,sbnv->bnvq', k, v * w[:, :, :, None])
            r = jax.nn.sigmoid(inp @ Wr_w.T + Wr_b)
            out = jnp.einsum('sbnq,bnvq->sbnv', q, A) * r[:, :, :, None]
            out = out.reshape(S, B, d)
            out = out @ Wo_w.T + Wo_b
            return (out, A)
        return _reference_tuple_inner(inp, Wq_w, Wq_b, Wk_w, Wk_b, Wv_w, Wv_b, Wo_w, Wo_b, Ww_w, Ww_b, Wr_w, Wr_b)[0]

    def _L1_ffn_ref(x, Wqkv, q_scale, k_scale, Wo, ln_g, ln_b, W1, b1, W2, b2):
        import jax, jax.numpy as jnp
        import numpy as np
        DIM = 128
        DEPTH = 6
        HEADS = 16
        DIM_HEAD = 64
        WINDOW = 32
        INNER = HEADS * DIM_HEAD
        DIM_INNER = int(DIM * 4 * 2 / 3)
        QK_SCALE = 8.0

        def shift_tokens(t):
            a, s = jnp.split(t, 2, -1)
            s = jnp.pad(s, ((0, 0), (1, 0), (0, 0)))[:, :-1]
            return jnp.concatenate([a, s], -1)

        def l2norm(t):
            return t / jnp.maximum(jnp.linalg.norm(t, axis=-1, keepdims=True), 1e-12)

        def rotate_half(x):
            x1, x2 = jnp.split(x, 2, -1)
            return jnp.concatenate([-x2, x1], -1)

        def rotary_tables(n):
            half = jnp.arange(0, DIM_HEAD, 2, dtype=jnp.float32)
            inv_freq = 1.0 / 10000.0 ** (half / DIM_HEAD)
            t = jnp.arange(n, dtype=jnp.float32)
            freqs = t[:, None] * inv_freq[None, :]
            freqs = jnp.concatenate([freqs, freqs], -1)
            base_scale = (half + 0.4 * DIM_HEAD) / (1.4 * DIM_HEAD)
            power = (t - n // 2) / (WINDOW // 2)
            scale = base_scale[None, :] ** power[:, None]
            scale = jnp.concatenate([scale, scale], -1)
            return (freqs, scale)

        def local_attention(q, k, v):
            b, h, n, d = q.shape
            w = WINDOW
            nw = n // w
            bq = q.reshape(b, h, nw, w, d)
            bk = k.reshape(b, h, nw, w, d)
            bv = v.reshape(b, h, nw, w, d)

            def look(t):
                p = jnp.pad(t, ((0, 0), (0, 0), (1, 0), (0, 0), (0, 0)))
                return jnp.concatenate([p[:, :, :nw], p[:, :, 1:]], axis=3)
            bk2, bv2 = (look(bk), look(bv))
            seq = jnp.arange(n).reshape(nw, w)
            seq_p = jnp.pad(seq, ((1, 0), (0, 0)), constant_values=-1)
            jt = jnp.concatenate([seq_p[:nw], seq_p[1:]], axis=1)
            it = seq[:, :, None]
            jb = jt[:, None, :]
            mask = (it < jb) | (it > jb + w) | (jb == -1)
            sim = jnp.einsum('bhwie,bhwje->bhwij', bq, bk2) * QK_SCALE
            sim = jnp.where(mask, -jnp.finfo(sim.dtype).max, sim)
            attn = jax.nn.softmax(sim, -1)
            out = jnp.einsum('bhwij,bhwje->bhwie', attn, bv2)
            return out.reshape(b, h, n, d)

        def attn_layer(x, Wqkv, qs, ksc, Wo):
            b, n, _ = x.shape
            qkv = x @ Wqkv
            q, k, v = jnp.split(qkv, 3, -1)
            sh = lambda t: t.reshape(b, n, HEADS, DIM_HEAD).transpose(0, 2, 1, 3)
            q, k, v = (sh(q), sh(k), sh(v))
            q = l2norm(q) * qs
            k = l2norm(k) * ksc
            freqs, scale = rotary_tables(n)
            cos, sin = (jnp.cos(freqs), jnp.sin(freqs))
            q = q * cos * scale + rotate_half(q) * sin * scale
            inv = 1.0 / scale
            k = k * cos * inv + rotate_half(k) * sin * inv
            out = local_attention(q, k, v)
            out = out.transpose(0, 2, 1, 3).reshape(b, n, INNER)
            return out @ Wo

        def ffn_layer(x, g, bln, W1, b1, W2, b2):
            mu = x.mean(-1, keepdims=True)
            var = ((x - mu) ** 2).mean(-1, keepdims=True)
            xn = (x - mu) / jnp.sqrt(var + 1e-05) * g + bln
            hg = xn @ W1 + b1
            a, gate = jnp.split(hg, 2, -1)
            return a * jax.nn.gelu(gate, approximate=False) @ W2 + b2
        for i in range(DEPTH):
            x = attn_layer(shift_tokens(x), Wqkv[i], q_scale[i], k_scale[i], Wo[i]) + x
            x = ffn_layer(shift_tokens(x), ln_g[i], ln_b[i], W1[i], b1[i], W2[i], b2[i]) + x
        return x
    x = L0_attn_x
    x = _layernorm(x + _L0_attn_ref(x, L0_attn_W_state, L0_attn_b_state, L0_attn_W_gate, L0_attn_b_gate), axis=-1)
    x = _layernorm(x + _L0_ffn_ref(x, L0_ffn_gate_w, L0_ffn_shared_gate, L0_ffn_shared_up, L0_ffn_shared_down, L0_ffn_r_gate, L0_ffn_r_up, L0_ffn_r_down), axis=-1)
    x = _layernorm(x + _L1_attn_ref(x, L1_attn_Wq_w, L1_attn_Wq_b, L1_attn_Wk_w, L1_attn_Wk_b, L1_attn_Wv_w, L1_attn_Wv_b, L1_attn_Wo_w, L1_attn_Wo_b, L1_attn_Ww_w, L1_attn_Ww_b, L1_attn_Wr_w, L1_attn_Wr_b), axis=-1)
    x = _layernorm(x + _L1_ffn_ref(x, L1_ffn_Wqkv, L1_ffn_q_scale, L1_ffn_k_scale, L1_ffn_Wo, L1_ffn_ln_g, L1_ffn_ln_b, L1_ffn_W1, L1_ffn_b1, L1_ffn_W2, L1_ffn_b2), axis=-1)
    return x

_drawn_inputs = setup_inputs


def setup_inputs(seed=0):
    import zlib

    import numpy as np

    out = dict(_drawn_inputs(seed))
    spreads = {'L1_ffn_q_scale': (1.0, 0.6),
     'L1_ffn_k_scale': (1.0, 0.6),
     'L1_ffn_ln_g': (1.0, 0.6),
     'L1_ffn_ln_b': (0.0, 0.8),
     'L1_ffn_b1': (0.0, 0.8),
     'L1_ffn_b2': (0.0, 0.1)}
    factors = {'L1_attn_Wq_b': 4.708,
     'L1_attn_Wk_b': 4.525,
     'L1_attn_Wv_b': 4.844,
     'L1_attn_Ww_b': 8.0,
     'L1_attn_Wr_b': 8.0,
     'L1_ffn_W1': 3.67,
     'L1_ffn_W2': 3.601}
    for name, (base, spread) in spreads.items():
        noise = np.random.default_rng([zlib.crc32(name.encode()), seed]).standard_normal(out[name].shape)
        drawn = base * np.exp(spread * noise) if base else spread * noise
        out[name] = jnp.asarray(drawn.astype(out[name].dtype))
    for name, factor in factors.items():
        out[name] = (out[name] * factor).astype(out[name].dtype)
    return out
```

```python
from contextlib import ExitStack

import numpy as np
import concourse.bass as bass
from concourse import mybir

F32 = mybir.dt.float32
I32 = mybir.dt.int32
ALU = mybir.AluOpType
ACT = mybir.ActivationFunctionType
X_AX = mybir.AxisListType.X

P = 128
NB, NT, C = 16, 256, 128
NC, W = 8, 32
N = NB * W
DEPTH, HEADS, DH = 6, 16, 64
INNER = HEADS * DH
DI = 341
FB = [128, 128, 85]
E = 8
MAGIC = 1597463007.0


class Tok:
    __slots__ = ("q", "at")

    def __init__(self, q, at):
        self.q, self.at = q, at


class Queue:

    def __init__(self, sem):
        self.sem, self.ops = sem, []

    def __call__(self, fn, *after):
        tok = Tok(self, len(self.ops))
        self.ops.append((fn, after))
        return tok


class Dmas:

    def __init__(self, sem):
        self.sem, self.n = sem, 0


def flat(after):
    for t in after:
        if isinstance(t, (list, tuple)):
            yield from flat(t)
        elif t is not None:
            yield t


def count_up(queues):
    named = {q: set() for q in queues}
    for q in queues:
        for _, after in q.ops:
            for t in flat(after):
                if t.q in named:
                    named[t.q].add(t.at)
    value = {}
    for q in queues:
        for n, at in enumerate(sorted(named[q])):
            value[(q, at)] = n + 1
    return value


def play(q, eng, value):
    seen = {}
    for i, (fn, after) in enumerate(q.ops):
        need = {}
        for t in flat(after):
            v = value[(t.q, t.at)] if isinstance(t.q, Queue) else t.at
            need[t.q] = max(v, need.get(t.q, 0))
        for src, v in need.items():
            if seen.get(src, 0) < v:
                eng.wait_ge(src.sem, v)
                seen[src] = v
        ins = fn(eng)
        if (q, i) in value:
            ins.then_inc(q.sem, 1)


def together(*gens):
    gens = list(gens)
    while gens:
        for g in list(gens):
            if next(g, gens) is gens:
                gens.remove(g)


def columns(sizes):
    at, out = 0, {}
    for name, n in sizes:
        out[name] = slice(at, at + n)
        at += n
    return out, at


KC, KC_N = columns([("ident", 128), ("center", 128), ("heads", 16), ("mean", 1), ("rank", 8), ("mask", 3 * 64)])
WA, WA_N = columns([("ws", 128), ("wg", 128), ("router", 8), ("sg", 256), ("su", 256), ("sd", 256),
                    ("eg", E * 256), ("eu", E * 256), ("ed", E * 256)])
WB, WB_N = columns([("wq", 128), ("wk", 128), ("ww", 128), ("wr", 128), ("wv", 8 * 128), ("wo", 128), ("perm", 8 * 128)])
BA, BA_N = columns([("bs", 1), ("bg", 1), ("bq", 1), ("bk", 1), ("bw", 1), ("br", 1), ("bv", 8), ("bo", 1)])


def program(nc, x_d, kc_d, wa_d, wb_d, ba_d, tab_d, qs_d, wqkv_d, wo_d, w1_d, w2_d, vec_d, out_d, keep_d):
    with ExitStack() as ctx:
        def sb(name, shape, dt=F32):
            return ctx.enter_context(nc.sbuf_tensor(name, shape, dt))

        def sem(name):
            return ctx.enter_context(nc.semaphore(name))

        bank = [ctx.enter_context(nc.psum_tensor(f"bank{i}", [P, 512], F32)) for i in range(8)]
        pe, dv, ac, po = (Queue(sem(n)) for n in ("s_pe", "s_dv", "s_ac", "s_po"))
        sp = Queue(sem("s_sp"))

        def dma(group, out, in_, *after):
            group.n += 16
            sp(lambda e: e.dma_start(out, in_).then_inc(group.sem, 16) and None, *after)
            return Tok(group, group.n)

        def mm(out, l, r, *after, st=True, sp_=True):
            return pe(lambda e: e.matmul(out, l, r, start=st, stop=sp_), *after)

        def tr(out, in_, *after):
            return pe(lambda e: e.transpose(out, in_, kc[:, KC["ident"]]), *after)

        def act(out, in_, f, *after, scale=1.0, bias=0.0):
            return ac(lambda e: e.activation(out, in_, f, scale=scale, bias=bias), *after)

        def tt(q, out, a, b, op, *after):
            return q(lambda e: e.tensor_tensor(out, a, b, op), *after)

        def stt(out, a, s, b, op0, op1, *after):
            return dv(lambda e: e.scalar_tensor_tensor(out, a, s, b, op0, op1), *after)

        def ts(out, a, s1, s2, op0, op1, *after):
            if op1 is None:
                return dv(lambda e: e.tensor_scalar(out, a, s1, None, op0), *after)
            return dv(lambda e: e.tensor_scalar(out, a, s1, s2, op0, op1), *after)

        def red(out, in_, op, *after):
            return dv(lambda e: e.tensor_reduce(out, in_, axis=X_AX, op=op), *after)

        class Ring:

            def __init__(self, banks):
                self.free_now, self.readers = list(banks), {b: [] for b in banks}

            def take(self):
                b = self.free_now.pop(0)
                return b, bank[b], self.readers[b]

            def free(self, b, *readers):
                self.readers[b] = list(readers)
                self.free_now.append(b)

        kc = sb("kc", [P, KC_N])
        ba = sb("ba", [P, BA_N])
        hb = sb("hb", [P, 3])
        Xr = sb("Xr", [P, NC, N])
        big0 = sb("big0", [P, 8192])
        big1 = sb("big1", [P, 8192])
        wqkv = sb("wqkv", [P, 2, 3 * INNER])
        wo = sb("wo", [P, 8, 128])
        w1 = sb("w1", [P, 2 * DI])
        w2 = sb("w2", [P, 3, 128])
        vec = sb("vec", [P, DEPTH, 9])
        tab = sb("tab", [P, 4, NC, DH])
        qsb = sb("qsb", [P, 4, DH])
        halo = sb("halo", [P, 2, NB])
        zero = sb("zero", [P, NB])
        xs = sb("xs", [P, 2, N])
        sq = sb("sq", [P, 2, 512])
        m1 = sb("m1", [P, 4, 512])
        m2 = sb("m2", [P, 2, 512])
        ss = sb("ss", [P, 2, 32])
        nw = sb("nw", [P, 2, 3, 128])
        qT = sb("qT", [P, 2, 8, P])
        S = sb("S", [P, 2, 1024])
        pT = sb("pT", [P, 2, 1024])
        On = sb("On", [P, 1, 1024])
        OT = sb("OT", [P, 1, 8, P])
        mx = sb("mx", [P, 2, 2, 16])
        rs = sb("rs", [P, 2, 2, 16])
        x2s = sb("x2s", [P, N])
        lc = sb("lc", [P, 3, N])
        ls = sb("ls", [P, 3, N])
        lv = sb("lv", [P, 3, 4])
        lr = sb("lr", [P, 3, 3, 4])
        xn = sb("xn", [P, N])
        gg = sb("gg", [P, 2, N])
        hh = sb("hh", [P, 3, N])

        ident = kc[:, KC["ident"]]

        g_kc, g_wa, g_vec, g_keep, g_out = (Dmas(sem(n)) for n in ("d_kc", "d_wa", "d_vec", "d_keep", "d_out"))
        g_x = [Dmas(sem(f"d_x{i}")) for i in range(2)]
        g_back = [Dmas(sem(f"d_back{i}")) for i in range(2)]
        g_big = [Dmas(sem(f"d_wqkv{i}")) for i in range(2)]
        g_wo, g_ffn, g_tab = Dmas(sem("d_wo")), Dmas(sem("d_ffn")), Dmas(sem("d_tab"))

        wa = big1
        t_kc = dma(g_kc, kc[:, :], kc_d)
        t_kc = dma(g_kc, ba[:, :], ba_d)
        t_x = []
        xin = [big0[:, 512 * i:512 * (i + 1)] for i in range(2)]
        wb = wqkv[:, 1, :]
        dma(g_wa, wa[:, 0:WA_N], wa_d)
        t_wa = dma(g_wa, wb[:, 0:WB_N], wb_d)

        def rsqrt(a, y, t, *after):
            k = dv(lambda e: e.tensor_scalar(t.bitcast(I32), a.bitcast(I32), 1, None, ALU.logical_shift_right), *after)
            k = dv(lambda e: e.tensor_scalar(y.bitcast(I32), t.bitcast(I32), -1.0, MAGIC, ALU.mult, ALU.add), k)
            for _ in range(3):
                k = tt(dv, t, y, y, ALU.mult, k)
                k = stt(t, t, -0.5, a, ALU.mult, ALU.mult, k)
                k = stt(y, t, 1.5, y, ALU.add, ALU.mult, k)
                yield
            return k

        def layernorm(ring, b, src, src_ready, last, busy):
            i, pb, free = ring.take()
            k = mm(pb[:, :], kc[:, KC["center"]], src, free, src_ready, t_kc)
            a1 = act(lc[:, b, :], pb[:, :], ACT.Copy, k, busy)
            a2 = act(ls[:, b, :], pb[:, :], ACT.Square, k, busy)
            ring.free(i, a1, a2)
            yield
            i, pb, free = ring.take()
            for j in range(4):
                k = mm(pb[:, j:j + 1], ls[:, b, 128 * j:128 * j + 128], kc[:, KC["mean"]], a2, free)
            k = ts(lv[:, b, :], pb[:, 0:4], 1e-5, None, ALU.add, None, k)
            ring.free(i, k)
            yield
            k = yield from rsqrt(lv[:, b, :], lr[:, b, 0, :], lr[:, b, 1, :], k)
            i, pb, free = ring.take()
            for j in range(4):
                k2 = mm(pb[:, 128 * j:128 * j + 128], lr[:, b, 0, j:j + 1].to_broadcast([P, P]), ident, k, free)
            k = last(lc[:, b, :], pb[:, :], [k2, a1])
            ring.free(i, k)
            yield
            return k

        ringA, ringO = Ring([0, 1, 2, 3, 4, 5]), Ring([6])
        V = lambda i: big0[:, 1024 + 512 * i:1536 + 512 * i]
        pP, tg, hist = V(0), V(1), [V(2), V(3)]
        x1, x2 = [V(4), V(5)], [V(6), V(7)]
        xe = [V(8), V(9)]
        hg = [V(10), V(11)]
        kw, qn, zr = V(12), V(13), [xs[:, 0, :], xs[:, 1, :]]
        rA, rB, rC = S[:, 0, 0:512], S[:, 0, 512:1024], S[:, 1, 0:512]
        q_s, k_s, tw, tq = pT[:, 0, 0:512], pT[:, 0, 512:1024], pT[:, 1, 0:512], pT[:, 1, 512:1024]
        sqq, sqk = On[:, 0, 0:512], On[:, 0, 512:1024]
        step_in = sb("step_in", [P, 2, NB])
        lg = sb("lg", [P, 4, 8])
        eqv = sb("eqv", [P, 4, 8])
        oh = sb("oh", [P, 4, 8])
        mxl = sb("mxl", [P, 3, 4])
        Ar = sb("Ar", [P, 2, W])
        bt = lambda ap: ap.rearrange("p (b t) -> p b t", b=NB)

        half = dv(lambda e: e.tensor_scalar(hb[:, 0:1], ba[:, BA["bg"]], 0.5, None, ALU.mult), t_kc)
        half = dv(lambda e: e.tensor_scalar(hb[:, 1:2], ba[:, BA["bw"]], 0.5, None, ALU.mult), t_kc)
        half = dv(lambda e: e.tensor_scalar(hb[:, 2:3], ba[:, BA["br"]], 0.5, None, ALU.mult), t_kc)
        t_zero = dv(lambda e: e.memset(zero[:, :], 0.0))

        st = {"scan": None, "x1": {}, "x2": {}, "x1_read": {}, "x2_read": {}, "xin_read": {}, "x": {}, "hist_read": {},
              "pP_read": None, "rA_read": None, "tg_read": None, "rB_read": None, "rC_read": None}

        def recurrence(c):
            t_in = dma(g_x[c % 2], xin[c % 2], x_d[:, c, :], st["xin_read"].get(c - 2))
            i, pb, free = ringA.take()
            k = mm(pb[:, :], wa[:, WA["ws"]], xin[c % 2], free, t_in, t_wa)
            kp = act(pP, pb[:, :], ACT.Identity, k, st["pP_read"], t_kc, bias=ba[:, BA["bs"]])
            ringA.free(i, kp)
            i, pb, free = ringA.take()
            k = mm(pb[:, :], wa[:, WA["wg"]], xin[c % 2], free)
            kg = act(tg, pb[:, :], ACT.Tanh, k, half, st["tg_read"], scale=0.5, bias=hb[:, 0:1])
            ringA.free(i, kg)
            yield
            h = bt(hist[c % 2])
            state = st["scan"]
            busy = st["hist_read"].get(c - 2)
            for t in range(W):
                if c == 0 and t == 0:
                    state = act(h[:, :, 0], bt(pP)[:, :, 0], ACT.Tanh, kp)
                    continue
                prev = h[:, :, t - 1] if t else bt(hist[(c - 1) % 2])[:, :, W - 1]
                k = tt(dv, step_in[:, t % 2, :], bt(pP)[:, :, t], prev, ALU.add, state, kp)
                state = act(h[:, :, t], step_in[:, t % 2, :], ACT.Tanh, k, busy)
                yield
            st["scan"], st["pP_read"] = state, k
            k1 = stt(rA, tg, 1.0, hist[c % 2], ALU.add, ALU.mult, state, kg, st["rA_read"])
            st["tg_read"] = k1
            k2 = stt(rA, rA, 0.5, xin[c % 2], ALU.mult, ALU.add, k1)
            st["xin_read"][c] = k2
            st["hist_read"][c] = k1
            yield
            last = lambda xc, rstd, w: tt(dv, x1[c % 2], xc, rstd, ALU.mult, w, st["x1_read"].get(c - 2))
            st["x1"][c] = st["rA_read"] = yield from layernorm(ringA, 0, rA, k2, last, st.get("ln0"))
            st["ln0"] = st["x1"][c]

        def experts(c):
            x, ready = x1[c % 2], st["x1"][c]
            i, pb, free = ringA.take()
            for j in range(4):
                k = mm(pb[:, 8 * j:8 * j + 8], x[:, 128 * j:128 * j + 128], wa[:, WA["router"]], free, ready)
            raw = pb[:, 0:32].rearrange("p (j e) -> p j e", e=8)
            k = dv(lambda e: e.tensor_copy(lg[:, :, :], raw), k, st.get("oh_read"))
            ringA.free(i, k)
            k = red(mxl[:, 0, :], lg[:, :, :], ALU.max, k)
            kt = act(mxl[:, 1, :], mxl[:, 0, :], ACT.Tanh, k, scale=0.5)
            mb = lambda n: mxl[:, n, :].unsqueeze(2).to_broadcast([P, 4, 8])
            k = tt(dv, eqv[:, :, :], lg[:, :, :], mb(0), ALU.is_equal, k)
            k = tt(dv, eqv[:, :, :], eqv[:, :, :], kc[:, KC["rank"]].unsqueeze(1).to_broadcast([P, 4, 8]), ALU.mult, k)
            k = red(mxl[:, 2, :], eqv[:, :, :], ALU.max, k)
            k = tt(dv, oh[:, :, :], eqv[:, :, :], mb(2), ALU.is_equal, k)
            k1 = ts(mxl[:, 1, :], mxl[:, 1, :], 0.5, 0.5, ALU.mult, ALU.add, kt)
            chosen = tt(dv, oh[:, :, :], oh[:, :, :], mb(1), ALU.mult, k, k1)
            yield
            acc, n = bank[7], 0
            acc_free = st.get("acc_read")
            for e in range(-1, E):
                if e < 0:
                    src, src_ready = x, ready
                    g0, u0, d0 = WA["sg"].start, WA["su"].start, WA["sd"].start
                else:
                    i, pb, free = ringA.take()
                    for j in range(4):
                        k = mm(pb[:, 128 * j:128 * j + 128], oh[:, j, e:e + 1].to_broadcast([P, P]), ident, free, chosen)
                    st["oh_read"] = k
                    src = xe[e % 2]
                    src_ready = tt(dv, src, x, pb[:, :], ALU.mult, k, st.get(("xe", e % 2)))
                    ringA.free(i, src_ready)
                    yield
                    g0, u0, d0 = (WA[s].start + 256 * e for s in ("eg", "eu", "ed"))
                for f in range(2):
                    ig, pg, free = ringA.take()
                    kg = mm(pg[:, :], wa[:, g0 + 128 * f:g0 + 128 * f + 128], src, free, src_ready)
                    iu, pu, free = ringA.take()
                    ku = mm(pu[:, :], wa[:, u0 + 128 * f:u0 + 128 * f + 128], src, free, src_ready)
                    if e >= 0:
                        st[("xe", e % 2)] = ku
                    h, was = hg[f], st.get(("hg", f))
                    ka = act(h, pg[:, :], ACT.Tanh, kg, was, scale=0.5)
                    k = stt(h, h, 1.0, pg[:, :], ALU.add, ALU.mult, ka, kg)
                    ringA.free(ig, k)
                    k = stt(h, h, 0.5, pu[:, :], ALU.mult, ALU.mult, k, ku)
                    ringA.free(iu, k)
                    yield
                    ka = mm(acc[:, :], wa[:, d0 + 128 * f:d0 + 128 * f + 128], h, k, acc_free, st=(n == 0), sp_=(n == 17))
                    st[("hg", f)] = ka
                    n += 1
            k = tt(dv, rB, acc[:, :], x, ALU.add, ka, ready, st["rB_read"])
            st["acc_read"] = st["x1_read"][c] = k
            yield
            last = lambda xc, rstd, w: tt(dv, x2[c % 2], xc, rstd, ALU.mult, w, st["x2_read"].get(c - 2))
            st["x2"][c] = st["rB_read"] = yield from layernorm(ringA, 1, rB, k, last, st.get("ln1"))
            st["ln1"] = st["x2"][c]

        def fast_weights(c):
            x, ready = x2[c % 2], st["x2"][c]
            done = st.get("fw_done")

            def project(w, f, out, scale, bias, extra=None):
                i, pb, free = ringA.take()
                k = mm(pb[:, :], wb[:, w], x, free, ready)
                k1 = act(out, pb[:, :], f, k, done, half, scale=scale, bias=bias)
                k2 = act(extra, pb[:, :], ACT.Square, k, done, scale=1.0, bias=bias) if extra is not None else None
                ringA.free(i, k1, k2)
                return k1, k2

            kq, kq2 = project(WB["wq"], ACT.Identity, q_s, 1.0, ba[:, BA["bq"]], sqq)
            yield
            kk, kk2 = project(WB["wk"], ACT.Identity, k_s, 1.0, ba[:, BA["bk"]], sqk)
            yield
            kw_, _ = project(WB["ww"], ACT.Tanh, tw, 0.5, hb[:, 1:2])
            kr_, _ = project(WB["wr"], ACT.Tanh, tq, 0.5, hb[:, 2:3])
            yield
            i, pb, free = ringA.take()
            for n, (s, w) in enumerate(((sqq, kq2), (sqk, kk2))):
                for j in range(4):
                    a = 16 * (4 * n + j)
                    k = mm(pb[:, a:a + 16], s[:, 128 * j:128 * j + 128], kc[:, KC["heads"]], w, free)
            nm, y, t = nw[:, 0, 0, :], nw[:, 0, 1, :], nw[:, 0, 2, :]
            k = ts(nm, pb[:, 0:128], 1e-24, None, ALU.max, None, k)
            ringA.free(i, k)
            yield
            k = yield from rsqrt(nm, y, t, k)
            wide = m2[:, :, :].rearrange("p a b -> p (a b)")
            k = dv(lambda e: e.tensor_copy(wide.rearrange("p (h d) -> p h d", d=8), y.unsqueeze(2).to_broadcast([P, 128, 8])),
                   k, st.get("wide_read"))
            out = []
            for n, (s, w, d) in enumerate(((q_s, kq, qn), (k_s, kk, kw))):
                i, pb, free = ringA.take()
                for j in range(4):
                    a = 128 * (4 * n + j)
                    k2 = mm(pb[:, 128 * j:128 * j + 128], wide[:, a:a + 128], ident, k, free)
                st["wide_read"] = k2
                out.append(tt(dv, d, s, pb[:, :], ALU.mult, k2, w, done))
                ringA.free(i, out[-1])
                yield
            kn = stt(kw, tw, 1.0, kw, ALU.add, ALU.mult, kw_, out[1])
            acc, ia = None, None
            ia, acc, acc_free = ringO.take()
            for r in range(8):
                i, pb, free = ringA.take()
                k = mm(pb[:, :], wb[:, WB["wv"].start + 128 * r:WB["wv"].start + 128 * r + 128], x, free, ready)
                pr = m1[:, r % 2, :]
                k = stt(pr, pb[:, :], ba[:, BA["bv"].start + r:BA["bv"].start + r + 1], kw, ALU.add, ALU.mult, k, kn)
                ringA.free(i, k)
                k = red(Ar[:, r % 2, :], pr.rearrange("p (s t) -> p t s", s=NB), ALU.add, k, st.get(("Ar", r % 2)))
                yield
                z = zr[r % 2]
                k = tt(po, bt(z), bt(qn), Ar[:, r % 2, :].unsqueeze(1).to_broadcast([P, NB, W]), ALU.mult, k, out[0],
                       st.get(("zr", r % 2)))
                st[("Ar", r % 2)] = k
                p0 = WB["perm"].start + 128 * r
                k = mm(acc[:, :], wb[:, p0:p0 + 128], z, k, acc_free, st=(r == 0), sp_=(r == 7))
                st[("zr", r % 2)] = k
                yield
            k = stt(tq, tq, 1.0, acc[:, :], ALU.add, ALU.mult, k, kr_)
            ringO.free(ia, k)
            i, pb, free = ringA.take()
            k = mm(pb[:, :], wb[:, WB["wo"]], tq, free, k)
            st["fw_done"] = k
            k = stt(rC, pb[:, :], ba[:, BA["bo"]], x, ALU.add, ALU.add, k, ready, st["rC_read"])
            ringA.free(i, k)
            st["x2_read"][c] = k
            yield
            last = lambda xc, rstd, w: tt(dv, Xr[:, c, :], xc, rstd, ALU.mult, w)
            k = yield from layernorm(ringA, 2, rC, k, last, st.get("ln2"))
            st["rC_read"] = st["ln2"] = st["x"][c] = k
            dma(g_keep, keep_d[:, c, :], Xr[:, c, :], k)

        for n in range(NC + 2):
            together(*([recurrence(n)] if n < NC else []), *([experts(n - 1)] if 0 <= n - 1 < NC else []),
                     *([fast_weights(n - 2)] if n >= 2 else []))

        phase = [st["x"][NC - 1], Tok(pe, len(pe.ops) - 1), Tok(ac, len(ac.ops) - 1), Tok(po, len(po.ops) - 1)]
        t_keep = Tok(g_keep, g_keep.n)

        kT = big0[:, :].rearrange("p (r b s t) -> p r b s t", r=8, b=NB, s=2)
        vv = big1[:, :].rearrange("p (s i n) -> p s i n", s=2, i=4)
        z0 = po(lambda e: e.memset(big0[:, :], 0.0), phase)
        z1 = po(lambda e: e.memset(big1[:, :], 0.0), phase)
        rg = Ring([0, 1, 2, 3])
        for b in rg.readers:
            rg.readers[b] = phase
        L = {}
        units = [(l, c) for l in range(DEPTH) for c in range(NC)]
        tiles = [(u, i) for u in range(len(units)) for i in range(4)]
        t_vec = dma(g_vec, vec[:, :, :], vec_d)
        xtok = dict(st["x"])
        fin = {}

        def load_qkv(l):
            L["wqkv", l] = dma(g_big[l % 2], wqkv[:, l % 2, :], wqkv_d[l], L.get(("qkv_read", l - 2)), phase)

        def load_rest(l):
            w = L.get(("wo_read", l - 1))
            L["wo", l] = dma(g_wo, wo[:, :, :], wo_d[l], w)

        def load_ffn(l):
            w = L.get(("ffn_read", l - 1))
            dma(g_ffn, w1[:, :], w1_d[l], w)
            L["ffn", l] = dma(g_ffn, w2[:, :, :], w2_d[l], w)

        def load_tables(l):
            w = L.get(("tab_read", l - 1))
            dma(g_tab, tab[:, :, :, :], tab_d, w)
            k = dma(g_tab, qsb[:, :, :], qs_d[l], w)
            for n in range(4):
                L["tab", l] = tt(po, tab[:, n, :, :], tab[:, n, :, :], qsb[:, n, :].unsqueeze(1).to_broadcast([P, NC, DH]),
                                 ALU.mult, k)

        def shifted(dst, c, kind, *after):
            v = Xr[:, c, :].rearrange("p (b t) -> p b t", b=NB)
            d = dst.rearrange("p (b t) -> p b t", b=NB)
            edge = zero if c == 0 else halo[:, kind, :]
            a = [act(dst[0:64, :], Xr[0:64, c, :], ACT.Copy, *after),
                 act(d[64:128, :, 1:W], v[64:128, :, 0:W - 1], ACT.Copy, *after),
                 act(d[64:128, :, 0], edge[64:128, :], ACT.Copy, *after, L.get(("halo", kind)), t_zero)]
            L["halo", kind] = act(halo[64:128, kind, :], v[64:128, :, W - 1], ACT.Copy, *after, a[-1])
            return a + [L["halo", kind]]

        def stage_a(g):
            u, i = tiles[g]
            l, c = units[u]
            if i == 0:
                if c == 0:
                    if l == 0:
                        load_qkv(0)
                        load_tables(0)
                        load_rest(0)
                        load_ffn(0)
                    else:
                        load_tables(l)
                if c == 1 and l + 1 < DEPTH:
                    load_qkv(l + 1)
                L["xs", u] = shifted(xs[:, u % 2, :], c, 0, xtok[c], L.get(("xs_read", u - 2)), phase)
            xt = xs[:, u % 2, 128 * i:128 * i + 128]
            wl = wqkv[:, l % 2, :]
            prods = []
            for part in range(4):
                isk, h8 = part // 2, part % 2
                col = INNER * isk + 512 * h8
                ib, pb, free = rg.take()
                k = mm(pb[:, :], xt, wl[:, col:col + 512], free, L["xs", u], L["wqkv", l])
                s3 = part % 2
                ks = act(sq[:, s3, :], pb[:, :], ACT.Square, k, L.get(("sq", s3)))
                ct, sn = tab[:, 2 * isk, c, :], tab[:, 2 * isk + 1, c, :]
                n1, n2 = part, part % 2
                o1 = m1[:, n1, :].rearrange("p (h d) -> p h d", d=DH)
                o2 = m2[:, n2, :].rearrange("p (h d) -> p h d", d=DH)
                pv = pb[:, :].rearrange("p (h d) -> p h d", d=DH)
                k1 = tt(dv, o1, pv, ct.unsqueeze(1).to_broadcast([P, 8, DH]), ALU.mult, k, ks, L["tab", l], L.get(("m1", n1)))
                k2 = tt(dv, o2[:, :, 0:32], pv[:, :, 32:64], sn[:, 0:32].unsqueeze(1).to_broadcast([P, 8, 32]), ALU.mult,
                        L.get(("m2", n2)))
                k2 = tt(dv, o2[:, :, 32:64], pv[:, :, 0:32], sn[:, 32:64].unsqueeze(1).to_broadcast([P, 8, 32]), ALU.mult)
                rg.free(ib, ks, k2)
                L["tab_read", l] = k2
                kr = red(ss[:, g % 2, 8 * part:8 * part + 8], sq[:, s3, :].rearrange("p (h d) -> p h d", d=DH), ALU.add, ks,
                         L.get(("ss", g % 2)))
                L["sq", s3] = kr
                ka = tt(po, m1[:, n1, :], m1[:, n1, :], m2[:, n2, :], ALU.add, k1, k2)
                L["m2", n2] = ka
                prods.append((n1, ka))
                yield
            nm, y, t = (nw[:, g % 2, n, 0:32] for n in range(3))
            k = ts(nm, ss[:, g % 2, :], 1e-24, None, ALU.max, None, kr, L.get(("nw", g % 2)))
            L["ss", g % 2] = k
            k = yield from rsqrt(nm, y, t, k)
            ready = []
            for part, (n1, ka) in enumerate(prods):
                o1 = m1[:, n1, :].rearrange("p (h d) -> p h d", d=DH)
                rb = y[:, 8 * part:8 * part + 8].unsqueeze(2).to_broadcast([P, 8, DH])
                ready.append((n1, tt(po, o1, o1, rb, ALU.mult, k, ka)))
            L["nw", g % 2] = ready[-1][1]
            L["rot", g] = ready
            yield
            for h8 in range(2):
                ib, pb, free = rg.take()
                col = 2 * INNER + 512 * h8
                k = mm(pb[:, :], xt, wl[:, col:col + 512], free)
                L["v", g, h8] = act(vv[:, c % 2, i, 512 * h8:512 * h8 + 512], pb[:, :], ACT.Copy, k, L.get(("av", g - 4)), z1)
                rg.free(ib, L["v", g, h8])
                yield
            L["xs_read", u] = k
            L["qkv_read", l] = k

        def stage_b(g):
            u, i = tiles[g]
            l, c = units[u]
            done = []
            for part, (n1, ready) in enumerate(L["rot", g]):
                isk, h8 = part // 2, part % 2
                ib, pb, free = rg.take()
                for j in range(4):
                    k = tr(pb[:, 128 * j:128 * j + 128], m1[:, n1, 128 * j:128 * j + 128], free, ready)
                L["m1", n1] = k
                if isk:
                    d = kT[:, 4 * h8:4 * h8 + 4, 4 * i:4 * i + 4, c % 2, :]
                    for j in range(4):
                        a = act(d[:, j], pb[:, 128 * j:128 * j + 128].rearrange("p (b t) -> p b t", b=4), ACT.Copy, k, z0,
                                L.get(("sim", g - 4)))
                else:
                    a = act(qT[:, g % 2, 4 * h8:4 * h8 + 4, :], pb[:, :].rearrange("p (r t) -> p r t", r=4), ACT.Copy, k,
                            L.get(("sim", g - 2)))
                rg.free(ib, a)
                done.append(a)
                yield
            L["T", g] = done

        def stage_c(g):
            u, i = tiles[g]
            l, c = units[u]
            msk = kc[:, KC["mask"]].rearrange("p (v k) -> p v k", v=3)[:, 0 if c == 0 else 1 + c % 2, :]
            s = g % 2
            Sv = S[:, s, :].rearrange("p (q r k) -> p q r k", q=2, r=8)
            ka = []
            for r in range(8):
                for par in range(2):
                    for b in range(4):
                        rows = slice(64 * par, 64 * par + 64)
                        k = mm(bank[4 + par][32 * b:32 * b + 32, 64 * r:64 * r + 64], qT[rows, s, r, 32 * b:32 * b + 32],
                               kT[rows, r, 4 * i + b, :, :].rearrange("p s t -> p (s t)"), L["T", g], L.get("sim_read"), z0)
            L["sim", g] = k
            yield
            for par in range(2):
                pv = bank[4 + par][:, :].rearrange("p (r k) -> p r k", r=8)
                ka.append(tt(dv, Sv[:, par], pv, msk.unsqueeze(1).to_broadcast([P, 8, 64]), ALU.add, k, L.get(("S", s)), phase))
            L["sim_read"] = ka[-1]
            S16 = S[:, s, :].rearrange("p (h k) -> p h k", h=16)
            k = red(mx[:, s, 0, :], S16, ALU.max, ka)
            yield
            k = tt(po, S16, S16, mx[:, s, 0, :].unsqueeze(2).to_broadcast([P, 16, 64]), ALU.subtract, k)
            kx = act(S[:, s, :], S[:, s, :], ACT.Exp, k)
            yield
            kt = dv(lambda e: e.transpose(pT[:, s, :], S[:, s, :]), kx, L.get(("av", g - 2)), phase)
            k = red(mx[:, s, 1, :], S16, ALU.add, kx)
            L["S", s] = [kt, k]
            L["sum", g] = dv(lambda e: e.reciprocal(rs[:, s, 0, :], mx[:, s, 1, :]), k)
            L["pT", g] = kt
            yield

        def stage_d(g):
            u, i = tiles[g]
            l, c = units[u]
            s = g % 2
            pv = pT[:, s, :].rearrange("p (q r m k) -> p q r m k", q=2, r=8, m=2)
            ko = []
            for par in range(2):
                for r in range(8):
                    h = 2 * r + par
                    for n, m in enumerate((1 - c % 2, c % 2)):
                        for b in range(4):
                            rows = slice(32 * b, 32 * b + 32)
                            k = mm(bank[6 + par][rows, 64 * r:64 * r + 64], pv[rows, par, r, m, :],
                                   vv[rows, m, i, 64 * h:64 * h + 64], L["pT", g], L["v", g, 0], L["v", g, 1],
                                   L.get(("o_read", par)), z1, st=(n == 0), sp_=(n == 1))
                o = On[:, 0, :].rearrange("p (r q d) -> p r q d", q=2, d=DH)[:, :, par, :]
                kk = tt(dv, o, bank[6 + par][:, :].rearrange("p (r d) -> p r d", d=DH),
                        rs[:, s, 0, 8 * par:8 * par + 8].unsqueeze(2).to_broadcast([P, 8, DH]), ALU.mult, k, L["sum", g],
                        L.get("On_read"))
                L["o_read", par] = kk
                ko.append(kk)
                yield
            L["av", g] = k
            L["On", g] = ko

        def stage_e(g):
            u, i = tiles[g]
            l, c = units[u]
            ko = []
            for h8 in range(2):
                ib, pb, free = rg.take()
                for j in range(4):
                    r = 4 * h8 + j
                    k = tr(pb[:, 128 * j:128 * j + 128], On[:, 0, 128 * r:128 * r + 128], free, L["On", g])
                a = act(OT[:, 0, 4 * h8:4 * h8 + 4, :], pb[:, :].rearrange("p (r t) -> p r t", r=4), ACT.Copy, k,
                        L.get("OT_read"))
                rg.free(ib, a)
                ko.append(a)
                yield
            L["On_read"] = k
            ib, pb, free = rg.take()
            for r in range(8):
                k = mm(pb[:, 0:128], wo[:, r, :], OT[:, 0, r, :], free, ko, L["wo", l], st=(r == 0), sp_=(r == 7))
            L["OT_read"] = k
            L["wo_read", l] = k
            xv = Xr[:, c, 128 * i:128 * i + 128]
            k = tt(dv, xv, pb[:, 0:128], xv, ALU.add, k, L["xs", u], xtok[c])
            rg.free(ib, k)
            L["res", u, i] = k
            yield
            if i == 3 and c == NC - 1 and l + 1 < DEPTH:
                load_rest(l + 1)

        def stage_f(u):
            l, c = units[u]
            v = lambda n, rows=P: vec[0:rows, l, n:n + 1]
            ready = [L["res", u, i] for i in range(4)]
            a = shifted(x2s[:, :], c, 1, ready, L.get("x2s_read"))
            yield

            def last(xc, rstd, w):
                k = tt(dv, xn[:, :], xc, rstd, ALU.mult, w, L.get("xn_read"))
                L["xn"] = act(xn[:, :], xn[:, :], ACT.Identity, k, t_vec, scale=v(7), bias=v(8))
                return k

            k = yield from layernorm(rg, 0, x2s[:, :], a, last, L.get("ln"))
            L["x2s_read"] = L["ln"] = k
            kh = []
            for f, rows in enumerate(FB):
                ig, pg, free = rg.take()
                kg = mm(pg[0:rows, :], w1[:, DI + 128 * f:DI + 128 * f + rows], xn[:, :], free, L["xn"], L["ffn", l])
                kg = act(gg[0:rows, f % 2, :], pg[0:rows, :], ACT.Gelu, kg, L.get(("gg", f % 2)), bias=v(3 + f, rows))
                rg.free(ig, kg)
                yield
                ia, pa, free = rg.take()
                ka = mm(pa[0:rows, :], w1[:, 128 * f:128 * f + rows], xn[:, :], free)
                k = stt(hh[0:rows, f, :], pa[0:rows, :], v(f, rows), gg[0:rows, f % 2, :], ALU.add, ALU.mult, ka, kg,
                        L.get("hh_read"))
                L["gg", f % 2] = k
                rg.free(ia, k)
                kh.append(k)
                yield
            L["xn_read"] = ka
            ib, pb, free = rg.take()
            for f, rows in enumerate(FB):
                k = mm(pb[:, :], w2[0:rows, f, :], hh[0:rows, f, :], free, kh, st=(f == 0), sp_=(f == 2))
            L["hh_read"] = L["ffn_read", l] = k
            k = stt(Xr[:, c, :], pb[:, :], v(6), Xr[:, c, :], ALU.add, ALU.add, k, a, ready)
            rg.free(ib, k)
            xtok[c] = k
            yield
            if c == NC - 1 and l + 1 < DEPTH:
                load_ffn(l + 1)
            if l == DEPTH - 1:
                b = c % 2
                kd = dma(g_back[b], xs2[b], keep_d[:, c, :], t_keep, fin.get(("back", b)))
                k = tt(dv, Xr[:, c, :], Xr[:, c, :], xs2[b], ALU.add, k, kd)
                fin["back", b] = k
                yield
                end = lambda xc, rstd, w: tt(dv, Xr[:, c, :], xc, rstd, ALU.mult, w)
                k = yield from layernorm(rg, 1, Xr[:, c, :], k, end, fin.get("ln"))
                fin["ln"] = k
                dma(g_out, out_d[:, c, :], Xr[:, c, :], k)

        xs2 = [lc[:, 2, :], ls[:, 2, :]]
        NG = len(tiles)
        F_now = []

        def pump(n):
            for _ in range(n):
                if F_now and next(F_now[0], F_now) is F_now:
                    F_now.pop(0)

        def run(gen):
            for _ in gen:
                pump(1)

        for g in range(-2, NG):
            if 0 <= g + 1 < NG:
                run(stage_b(g + 1))
            if g + 2 < NG:
                run(stage_a(g + 2))
            if g >= 0:
                run(stage_d(g))
            if 0 <= g + 1 < NG:
                run(stage_c(g + 1))
            if g >= 0:
                run(stage_e(g))
                if tiles[g][1] == 3:
                    while F_now:
                        pump(1)
                    F_now.append(stage_f(tiles[g][0]))
        while F_now:
            pump(1)
        sp(lambda e: None, Tok(g_out, g_out.n), Tok(g_keep, g_keep.n))

        value = count_up([pe, dv, ac, po, sp])
        block = ctx.enter_context(nc.Block())

        def play_dma(q, eng):
            seen = {}
            for fn, after in q.ops:
                for t in flat(after):
                    v = value[(t.q, t.at)] if isinstance(t.q, Queue) else t.at
                    if seen.get(t.q, 0) < v:
                        eng.wait_ge(t.q.sem, v)
                        seen[t.q] = v
                fn(eng)

        @block.sync
        def _(eng):
            play_dma(sp, eng)

        @block.tensor
        def _(eng):
            play(pe, eng, value)

        @block.vector
        def _(eng):
            play(dv, eng, value)

        @block.scalar
        def _(eng):
            play(ac, eng, value)

        @block.gpsimd
        def _(eng):
            play(po, eng, value)


def shape_constants():
    f = np.float32
    kc, perm = np.zeros((P, KC_N), f), np.zeros((P, 8 * P), f)
    kc[:, KC["ident"]] = np.eye(P, dtype=f)
    kc[:, KC["center"]] = np.eye(P, dtype=f) - f(1.0 / P)
    n = np.arange(P)
    for r in range(8):
        m = np.zeros((P, P), f)
        m[n, 8 * (n // 8) + (n % 8 + r) % 8] = 0.25
        perm[:, P * r:P * r + P] = m
    kc[n, KC["heads"].start + n // 8] = 1.0
    kc[:, KC["mean"]] = 1.0 / P
    kc[:, KC["rank"]] = np.arange(8, 0, -1)
    low = f(-np.finfo(f).max)
    a, b = (n % W)[:, None], np.arange(W)[None, :]
    cur, prev = np.where(b <= a, f(0), low), np.where(b >= a, f(0), low)
    none = np.full((P, W), low, f)
    kc[:, KC["mask"]] = np.concatenate([cur, none, cur, prev, prev, cur], 1)
    half = np.arange(0, DH, 2, dtype=f)
    inv = (f(1.0) / np.power(f(10000.0), half / f(DH))).astype(f)
    t = np.arange(NT, dtype=f)
    fr = t[:, None] * inv[None, :]
    fr = np.concatenate([fr, fr], -1).astype(np.float64)
    base = ((half + f(0.4 * DH)) / f(1.4 * DH)).astype(f)
    power = (t - f(NT // 2)) / f(W // 2)
    sc = np.power(base[None, :].astype(np.float64), power[:, None].astype(np.float64))
    sc = np.concatenate([sc, sc], -1)
    sign = np.concatenate([-np.ones(DH // 2), np.ones(DH // 2)])
    tabs = np.stack([8.0 * np.cos(fr) * sc, 8.0 * np.sin(fr) * sc * sign, np.cos(fr) / sc, np.sin(fr) / sc * sign])
    tabs = tabs.reshape(4, NC, W, DH).transpose(2, 0, 1, 3)
    return kc, perm, np.tile(tabs, (4, 1, 1, 1)).astype(f)


def kernel(**inputs):
    import concourse.bacc as bacc
    from concourse.bass_utils import run_bass_kernel_spmd

    a = {k: np.asarray(v) for k, v in inputs.items()}
    f = np.float32
    kc, perm, tabs = shape_constants()
    rot = lambda w, r: np.concatenate([np.roll(w[8 * h:8 * h + 8], -r, 0) for h in range(16)])
    A = lambda n: a["L1_attn_" + n]
    down = lambda w: w.T.reshape(2, 128, 128).transpose(1, 0, 2).reshape(128, 256)
    wa = np.zeros((P, WA_N), f)
    put = {"ws": a["L0_attn_W_state"].T, "wg": a["L0_attn_W_gate"].T, "router": a["L0_ffn_gate_w"].T,
           "sg": a["L0_ffn_shared_gate"].T, "su": a["L0_ffn_shared_up"].T, "sd": down(a["L0_ffn_shared_down"]),
           "eg": a["L0_ffn_r_gate"].transpose(2, 0, 1).reshape(128, -1),
           "eu": a["L0_ffn_r_up"].transpose(2, 0, 1).reshape(128, -1),
           "ed": np.concatenate([down(w) for w in a["L0_ffn_r_down"]], 1),
           "wq": A("Wq_w").T, "wk": A("Wk_w").T, "ww": np.repeat(A("Ww_w").T, 8, 1), "wr": np.repeat(A("Wr_w").T, 8, 1),
           "wv": np.concatenate([rot(A("Wv_w"), r).T for r in range(8)], 1), "wo": A("Wo_w").T}
    wb = np.zeros((P, WB_N), f)
    put["perm"] = perm
    for n, w in put.items():
        if n in WA:
            wa[:, WA[n]] = w
        else:
            wb[:, WB[n]] = w
    ba = np.zeros((P, BA_N), f)
    put = {"bs": a["L0_attn_b_state"][:, None], "bg": a["L0_attn_b_gate"][:, None], "bq": A("Wq_b")[:, None],
           "bk": A("Wk_b")[:, None], "bw": np.repeat(A("Ww_b"), 8)[:, None], "br": np.repeat(A("Wr_b"), 8)[:, None],
           "bv": np.stack([rot(A("Wv_b"), r) for r in range(8)], 1), "bo": A("Wo_b")[:, None]}
    for n, w in put.items():
        ba[:, BA[n]] = w
    B = lambda n: a["L1_ffn_" + n]
    swap = lambda s: np.concatenate([s[:, 32:], s[:, :32]], 1)
    qs = np.stack([B("q_scale"), swap(B("q_scale")), B("k_scale"), swap(B("k_scale"))], 1)
    qs = np.ascontiguousarray(np.broadcast_to(qs[:, None], (DEPTH, P, 4, DH)))
    w2 = np.zeros((DEPTH, 3 * P, C), f)
    w2[:, :DI] = B("W2")
    vec = np.zeros((P, DEPTH, 9), f)
    for l in range(DEPTH):
        for n in range(2):
            for m, rows in enumerate(FB):
                vec[:rows, l, 3 * n + m] = B("b1")[l, DI * n + 128 * m:DI * n + 128 * m + rows]
        vec[:, l, 6], vec[:, l, 7], vec[:, l, 8] = B("b2")[l], B("ln_g")[l], B("ln_b")[l]
    arrays = {
        "x": a["L0_attn_x"].reshape(NB, NC, W, C).transpose(3, 1, 0, 2).reshape(C, NC, N),
        "kc": kc, "wa": wa, "wb": wb, "ba": ba, "tab": tabs, "qs": qs, "wqkv": B("Wqkv"),
        "wo": B("Wo").reshape(DEPTH, 8, 128, C).transpose(0, 2, 1, 3), "w1": B("W1"),
        "w2": w2.reshape(DEPTH, 3, P, C).transpose(0, 2, 1, 3), "vec": vec,
    }
    nc = bacc.Bacc("TRN2", target_bir_lowering=False, num_devices=1)
    ins, args = {}, []
    for n, v in arrays.items():
        v = np.ascontiguousarray(v)
        ins["in_" + n] = v
        args.append(nc.dram_tensor("in_" + n, v.shape, F32, kind="ExternalInput").ap())
    out = nc.dram_tensor("out", (C, NC, N), F32, kind="ExternalOutput").ap()
    keep = nc.dram_tensor("keep", (C, NC, N), F32, kind="Internal").ap()
    program(nc, *args, out, keep)
    r = run_bass_kernel_spmd(nc, [ins], core_ids=[0])
    y = np.asarray(r.results[0]["out"])
    return np.ascontiguousarray(y.reshape(C, NC, NB, W).transpose(2, 1, 3, 0)).reshape(NB, NT, C)
```

```python
from contextlib import ExitStack

import numpy as np
import concourse.bass as bass
from concourse import mybir

F32 = mybir.dt.float32
I32 = mybir.dt.int32
ALU = mybir.AluOpType
ACT = mybir.ActivationFunctionType
X_AX = mybir.AxisListType.X

P = 128
NB, NT, C = 16, 256, 128
NC, W = 8, 32
N = NB * W
DEPTH, HEADS, DH = 6, 16, 64
INNER = HEADS * DH
DI = 341
FB = [128, 128, 85]
E = 8
MAGIC = 1597463007.0


class Tok:
    __slots__ = ("q", "at", "t")

    def __init__(self, q, at, t):
        self.q, self.at, self.t = q, at, t


class Queue:

    def __init__(self, sem):
        self.sem, self.ops, self.clock = sem, [], 0.0

    def __call__(self, fn, cost, *after):
        start = max([self.clock] + [t.t + 0.1 for t in flat(after)])
        self.clock = start + cost
        tok = Tok(self, len(self.ops), self.clock)
        self.ops.append((fn, after))
        return tok


class Dmas:

    def __init__(self, sem):
        self.sem, self.n = sem, 0


def flat(after):
    for t in after:
        if isinstance(t, (list, tuple)):
            yield from flat(t)
        elif t is not None:
            yield t


def count_up(queues):
    named = {q: set() for q in queues}
    for q in queues:
        for _, after in q.ops:
            for t in flat(after):
                if t.q in named:
                    named[t.q].add(t.at)
    value = {}
    for q in queues:
        for n, at in enumerate(sorted(named[q])):
            value[(q, at)] = n + 1
    return value


def play(q, eng, value):
    seen = {}
    for i, (fn, after) in enumerate(q.ops):
        need = {}
        for t in flat(after):
            v = value[(t.q, t.at)] if isinstance(t.q, Queue) else t.at
            need[t.q] = max(v, need.get(t.q, 0))
        for src, v in need.items():
            if seen.get(src, 0) < v:
                eng.wait_ge(src.sem, v)
                seen[src] = v
        ins = fn(eng)
        if (q, i) in value:
            ins.then_inc(q.sem, 1)


def take_turns(lanes, known):
    ahead = {}
    lanes = list(lanes)
    for g in list(lanes):
        ahead[g] = next(g, None)
    while True:
        best = None
        for g in lanes:
            if ahead[g] is None:
                continue
            rank, q, needs = ahead[g]
            t = q.clock
            for n in needs:
                if isinstance(n, Ring):
                    n = n.soonest()
                elif isinstance(n, tuple):
                    n = known.get(n, False)
                if n is False:
                    t = None
                    break
                for x in flat([n]):
                    t = max(t, x.t + 0.1)
            if t is not None and (best is None or (t, rank) < best[:2]):
                best = (t, rank, g)
        if best is None:
            assert all(ahead[g] is None for g in lanes), [ahead[g] for g in lanes]
            return
        soon = best[0] + 0.15
        for g in lanes:
            if ahead[g] is None or g is best[2]:
                continue
            rank, q, needs = ahead[g]
            if rank >= best[1]:
                continue
            t = q.clock
            for n in needs:
                if isinstance(n, Ring):
                    n = n.soonest()
                elif isinstance(n, tuple):
                    n = known.get(n, False)
                if n is False:
                    t = None
                    break
                for x in flat([n]):
                    t = max(t, x.t + 0.1)
            if t is not None and t <= soon:
                best = (t, rank, g)
        ahead[best[2]] = next(best[2], None)


class Ring:

    def __init__(self, bank, banks):
        self.bank, self.free_now, self.readers = bank, list(banks), {b: [] for b in banks}

    def when(self, b):
        return max([t.t for t in flat(self.readers[b])], default=0.0)

    def soonest(self):
        if not self.free_now:
            return False
        return self.readers[min(self.free_now, key=self.when)]

    def take(self):
        b = min(self.free_now, key=self.when)
        self.free_now.remove(b)
        return b, self.bank[b], self.readers[b]

    def free(self, b, *readers):
        self.readers[b] = list(readers)
        self.free_now.append(b)


def columns(sizes):
    at, out = 0, {}
    for name, n in sizes:
        out[name] = slice(at, at + n)
        at += n
    return out, at


KC, KC_N = columns([("ident", 128), ("center", 128), ("heads", 16), ("mean", 1), ("rank", 8), ("mask", 3 * 64)])
WA, WA_N = columns([("ws", 128), ("wg", 128), ("router", 8), ("sg", 256), ("su", 256), ("sd", 256),
                    ("eg", E * 256), ("eu", E * 256), ("ed", E * 256)])
WB, WB_N = columns([("wq", 128), ("wk", 128), ("ww", 128), ("wr", 128), ("wv", 8 * 128), ("wo", 128), ("perm", 8 * 128)])
BA, BA_N = columns([("bs", 1), ("bg", 1), ("bq", 1), ("bk", 1), ("bw", 1), ("br", 1), ("bv", 8), ("bo", 1)])


def program(nc, x_d, kc_d, wa_d, wb_d, ba_d, tab_d, qs_d, wqkv_d, wo_d, w1_d, w2_d, vec_d, out_d, keep_d):
    with ExitStack() as ctx:
        def sb(name, shape, dt=F32):
            return ctx.enter_context(nc.sbuf_tensor(name, shape, dt))

        def sem(name):
            return ctx.enter_context(nc.semaphore(name))

        bank = [ctx.enter_context(nc.psum_tensor(f"bank{i}", [P, 512], F32)) for i in range(8)]
        pe, dv, ac, po = (Queue(sem(n)) for n in ("s_pe", "s_dv", "s_ac", "s_po"))
        sp = Queue(sem("s_sp"))

        def size(ap):
            n = 1
            for d in ap.shape[1:]:
                n *= d
            return n

        def dma(group, out, in_, *after):
            group.n += 16
            k = sp(lambda e: e.dma_start(out, in_).then_inc(group.sem, 16) and None, 0.65, *after)
            return Tok(group, group.n, k.t + 2.0)

        def mm(out, l, r, *after, st=True, sp_=True):
            n, m = size(r), size(l)
            cost = max(0.05, n * 2 * 2 / 2400) if m <= 64 else max(0.107, n * 2 * 2 / 2400)
            return pe(lambda e: e.matmul(out, l, r, start=st, stop=sp_), cost, *after)

        def tr(out, in_, *after):
            return pe(lambda e: e.transpose(out, in_, kc[:, KC["ident"]]), 0.107, *after)

        def act(out, in_, f, *after, scale=1.0, bias=0.0):
            return ac(lambda e: e.activation(out, in_, f, scale=scale, bias=bias), 0.06 + size(out) / 1200, *after)

        def tt(q, out, a, b, op, *after):
            n = size(out)
            return q(lambda e: e.tensor_tensor(out, a, b, op), 0.066 + n / 960 if q is dv else 0.1 + 0.0021 * n, *after)

        def stt(out, a, s, b, op0, op1, *after):
            return dv(lambda e: e.scalar_tensor_tensor(out, a, s, b, op0, op1), 0.1 + size(out) / 960, *after)

        def ts(out, a, s1, s2, op0, op1, *after):
            cost = 0.066 + size(out) / 960
            if op1 is None:
                return dv(lambda e: e.tensor_scalar(out, a, s1, None, op0), cost, *after)
            return dv(lambda e: e.tensor_scalar(out, a, s1, s2, op0, op1), cost, *after)

        def red(out, in_, op, *after):
            return dv(lambda e: e.tensor_reduce(out, in_, axis=X_AX, op=op), 0.066 + size(in_) / 960, *after)

        kc = sb("kc", [P, KC_N])
        ba = sb("ba", [P, BA_N])
        hb = sb("hb", [P, 3])
        Xr = sb("Xr", [P, NC, N])
        big0 = sb("big0", [P, 8192])
        big1 = sb("big1", [P, 8192])
        wqkv = sb("wqkv", [P, 2, 3 * INNER])
        wo = sb("wo", [P, 8, 128])
        w1 = sb("w1", [P, 2 * DI])
        w2 = sb("w2", [P, 3, 128])
        vec = sb("vec", [P, DEPTH, 9])
        tab = sb("tab", [P, 4, NC, DH])
        qsb = sb("qsb", [P, 4, DH])
        halo = sb("halo", [P, 2, NB])
        zero = sb("zero", [P, NB])
        xs = sb("xs", [P, 2, N])
        sq = sb("sq", [P, 2, 512])
        m1 = sb("m1", [P, 4, 512])
        m2 = sb("m2", [P, 2, 512])
        ss = sb("ss", [P, 2, 32])
        nw = sb("nw", [P, 2, 3, 32])
        qT = sb("qT", [P, 2, 8, P])
        S = sb("S", [P, 2, 1024])
        On = sb("On", [P, 1, 1024])
        OT = sb("OT", [P, 2, 8, P])
        vst = sb("vst", [P, 2, 512])
        P2 = sb("P2", [P, 8, P])
        mx = sb("mx", [P, 2, 2, 16])
        rs = sb("rs", [P, 2, 2, 16])
        x2s = sb("x2s", [P, N])
        lc = sb("lc", [P, N])
        ls = sb("ls", [P, N])
        back = sb("back", [P, N])
        lv = sb("lv", [P, 3, 4])
        lr = sb("lr", [P, 3, 3, 4])
        xn = sb("xn", [P, N])
        gg = sb("gg", [P, 3, N])
        hh = sb("hh", [P, 3, N])

        ident = kc[:, KC["ident"]]

        g_kc, g_wa, g_vec, g_keep, g_out = (Dmas(sem(n)) for n in ("d_kc", "d_wa", "d_vec", "d_keep", "d_out"))
        g_x = [Dmas(sem(f"d_x{i}")) for i in range(2)]
        g_back = [Dmas(sem(f"d_back{i}")) for i in range(2)]
        g_big = [Dmas(sem(f"d_wqkv{i}")) for i in range(2)]
        g_v = [Dmas(sem(f"d_v{i}")) for i in range(4)]
        g_wo, g_ffn, g_tab = Dmas(sem("d_wo")), Dmas(sem("d_ffn")), Dmas(sem("d_tab"))

        wa = big1
        t_kc = dma(g_kc, kc[:, :], kc_d)
        t_kc = dma(g_kc, ba[:, :], ba_d)
        t_x = []
        xin = [big0[:, 512 * i:512 * (i + 1)] for i in range(2)]
        wb = wqkv[:, 1, :]
        dma(g_wa, wa[:, 0:WA_N], wa_d)
        t_wa = dma(g_wa, wb[:, 0:WB_N], wb_d)

        def rsqrt(rank, a, y, t, *after):
            n = size(a) / 960 + 0.066
            k = dv(lambda e: e.tensor_scalar(t.bitcast(I32), a.bitcast(I32), 1, None, ALU.logical_shift_right), n, *after)
            yield rank, dv, [k]
            k = dv(lambda e: e.tensor_scalar(y.bitcast(I32), t.bitcast(I32), -1.0, MAGIC, ALU.mult, ALU.add), n, k)
            for _ in range(3):
                yield rank, dv, [k]
                k = tt(dv, t, y, y, ALU.mult, k)
                yield rank, dv, [k]
                k = stt(t, t, -0.5, a, ALU.mult, ALU.mult, k)
                yield rank, dv, [k]
                k = stt(y, t, 1.5, y, ALU.add, ALU.mult, k)
            return k

        LN = [(lc[:, :], ls[:, :]), (gg[:, 0, :], gg[:, 1, :]), (hh[:, 0, :], hh[:, 1, :])]

        def layernorm(rank, ring, b, src, src_ready, last, busy):
            bc, bs = LN[b]
            yield rank, pe, [ring, src_ready]
            i, pb, free = ring.take()
            k = mm(pb[:, :], kc[:, KC["center"]], src, free, src_ready, t_kc)
            yield rank, ac, [k, busy]
            a1 = act(bc, pb[:, :], ACT.Copy, k, busy)
            a2 = act(bs, pb[:, :], ACT.Square, k, busy)
            ring.free(i, a1, a2)
            yield rank, pe, [ring, a2]
            i, pb, free = ring.take()
            for j in range(4):
                k = mm(pb[:, j:j + 1], bs[:, 128 * j:128 * j + 128], kc[:, KC["mean"]], a2, free)
            yield rank, dv, [k]
            k = ts(lv[:, b, :], pb[:, 0:4], 1e-5, None, ALU.add, None, k)
            ring.free(i, k)
            yield rank, dv, [k]
            k = yield from rsqrt(rank, lv[:, b, :], lr[:, b, 0, :], lr[:, b, 1, :], k)
            yield rank, pe, [ring, k]
            i, pb, free = ring.take()
            for j in range(4):
                k2 = mm(pb[:, 128 * j:128 * j + 128], lr[:, b, 0, j:j + 1].to_broadcast([P, P]), ident, k, free)
            yield rank, dv, [k2, a1]
            k = last(bc, pb[:, :], [k2, a1])
            ring.free(i, k)
            return k

        ringA = Ring(bank, [0, 1, 2, 3, 4, 5])
        V = lambda i: big0[:, 1024 + 512 * i:1536 + 512 * i]
        pP, tg, hist = V(0), V(1), [V(2), V(3)]
        x1, x2 = [V(4), V(5)], [V(6), V(7)]
        xe = [V(8), V(9)]
        hg = [V(10), V(11)]
        kw, qn, zr = V(12), V(13), [xs[:, 0, :], xs[:, 1, :]]
        rA, rB, rC = S[:, 0, 0:512], S[:, 0, 512:1024], S[:, 1, 0:512]
        q_s, k_s, tw, tq = OT[:, 0, 0:4, :].rearrange("p a b -> p (a b)"), OT[:, 0, 4:8, :].rearrange("p a b -> p (a b)"), vst[:, 0, :], vst[:, 1, :]
        sqq, sqk = On[:, 0, 0:512], On[:, 0, 512:1024]
        step_in = sb("step_in", [P, 2, NB])
        lg = sb("lg", [P, 4, 8])
        eqv = sb("eqv", [P, 4, 8])
        oh = sb("oh", [P, 4, 8])
        mxl = sb("mxl", [P, 3, 4])
        Ar = sb("Ar", [P, 2, W])
        bt = lambda ap: ap.rearrange("p (b t) -> p b t", b=NB)

        for n, name in enumerate(("bg", "bw", "br")):
            half = ts(hb[:, n:n + 1], ba[:, BA[name]], 0.5, None, ALU.mult, None, t_kc)
        t_zero = dv(lambda e: e.memset(zero[:, :], 0.0), 0.1)

        st = {}

        def K(when, *key):
            return key if when else None

        def recurrence():
            state = None
            for c in range(NC):
                x = xin[c % 2]
                yield c, sp, [K(c >= 2, "u0", c - 2)]
                t_in = dma(g_x[c % 2], x, x_d[:, c, :], st.get(("u1", c - 2)))
                yield c, pe, [t_in, t_wa, ringA]
                i, pb, free = ringA.take()
                k = mm(pb[:, :], wa[:, WA["ws"]], x, free, t_in, t_wa)
                yield c, ac, [k]
                kp = act(pP, pb[:, :], ACT.Identity, k, st.get(("pP", c - 1)), t_kc, bias=ba[:, BA["bs"]])
                ringA.free(i, kp)
                yield c, pe, [ringA]
                i, pb, free = ringA.take()
                k = mm(pb[:, :], wa[:, WA["wg"]], x, free)
                yield c, ac, [k, K(c, "u0", c - 1)]
                kg = act(tg, pb[:, :], ACT.Tanh, k, half, st.get(("u0", c - 1)), scale=0.5, bias=hb[:, 0:1])
                ringA.free(i, kg)
                h = bt(hist[c % 2])
                busy = st.get(("u0", c - 2))
                for t in range(W):
                    if c == 0 and t == 0:
                        yield c, ac, [kp]
                        state = act(h[:, :, 0], bt(pP)[:, :, 0], ACT.Tanh, kp)
                        continue
                    prev = h[:, :, t - 1] if t else bt(hist[(c - 1) % 2])[:, :, W - 1]
                    yield -1, dv, [state, kp]
                    k = tt(dv, step_in[:, t % 2, :], bt(pP)[:, :, t], prev, ALU.add, state, kp)
                    yield -1, ac, [k]
                    state = act(h[:, :, t], step_in[:, t % 2, :], ACT.Tanh, k, busy)
                st["pP", c] = k
                st["hist", c] = state
                st["kg", c] = kg

        def first_norm():
            for c in range(NC):
                yield c, dv, [("hist", c)]
                k1 = stt(rA, tg, 1.0, hist[c % 2], ALU.add, ALU.mult, st["hist", c], st["kg", c], st.get(("x1", c - 1)))
                st["u0", c] = k1
                yield c, dv, [k1]
                k2 = stt(rA, rA, 0.5, xin[c % 2], ALU.mult, ALU.add, k1)
                st["u1", c] = k2
                yield c, dv, [K(c >= 2, "x1_read", c - 2)]
                last = lambda xc, rstd, w: tt(dv, x1[c % 2], xc, rstd, ALU.mult, w, st.get(("x1_read", c - 2)))
                st["x1", c] = yield from layernorm(c, ringA, 0, rA, k2, last, st.get(("x1", c - 1)))

        def experts():
            for c in range(NC):
                x = x1[c % 2]
                yield c, pe, [("x1", c), ringA]
                ready = st["x1", c]
                i, pb, free = ringA.take()
                for j in range(4):
                    k = mm(pb[:, 8 * j:8 * j + 8], x[:, 128 * j:128 * j + 128], wa[:, WA["router"]], free, ready)
                yield c, dv, [k]
                raw = pb[:, 0:32].rearrange("p (j e) -> p j e", e=8)
                k = dv(lambda e, raw=raw: e.tensor_copy(lg[:, :, :], raw), 0.1, k)
                ringA.free(i, k)
                yield c, dv, [k]
                k = red(mxl[:, 0, :], lg[:, :, :], ALU.max, k)
                yield c, ac, [k]
                kt = act(mxl[:, 1, :], mxl[:, 0, :], ACT.Tanh, k, scale=0.5)
                mb = lambda n: mxl[:, n, :].unsqueeze(2).to_broadcast([P, 4, 8])
                yield c, dv, [k]
                k = tt(dv, eqv[:, :, :], lg[:, :, :], mb(0), ALU.is_equal, k)
                yield c, dv, [k]
                k = tt(dv, eqv[:, :, :], eqv[:, :, :], kc[:, KC["rank"]].unsqueeze(1).to_broadcast([P, 4, 8]), ALU.mult, k)
                yield c, dv, [k]
                k = red(mxl[:, 2, :], eqv[:, :, :], ALU.max, k)
                yield c, dv, [k]
                k = tt(dv, oh[:, :, :], eqv[:, :, :], mb(2), ALU.is_equal, k, st.get("oh_read"))
                yield c, dv, [k, kt]
                k1 = ts(mxl[:, 1, :], mxl[:, 1, :], 0.5, 0.5, ALU.mult, ALU.add, kt)
                yield c, dv, [k, k1]
                chosen = tt(dv, oh[:, :, :], oh[:, :, :], mb(1), ALU.mult, k, k1)
                acc, n = bank[7], 0
                acc_free = st.get("acc_read")

                def down(e, f, h, k):
                    nonlocal n
                    d = WA["sd"].start if e < 0 else WA["ed"].start + 256 * e
                    ka = mm(acc[:, :], wa[:, d + 128 * f:d + 128 * f + 128], h, k, acc_free, st=(n == 0), sp_=(n == 17))
                    n += 1
                    return ka

                for e in range(-1, E):
                    if e < 0:
                        src, src_ready = x, ready
                        g0, u0 = WA["sg"].start, WA["su"].start
                    else:
                        yield c, pe, [ringA, chosen]
                        i, pb, free = ringA.take()
                        for j in range(4):
                            k = mm(pb[:, 128 * j:128 * j + 128], oh[:, j, e:e + 1].to_broadcast([P, P]), ident, free, chosen)
                        st["oh_read"] = k
                        yield c, dv, [k]
                        src = xe[e % 2]
                        src_ready = tt(dv, src, x, pb[:, :], ALU.mult, k, st.get(("xe", e % 2)))
                        ringA.free(i, src_ready)
                        g0, u0 = (WA[s].start + 256 * e for s in ("eg", "eu"))
                    for f in range(2):
                        yield c, pe, [ringA, src_ready]
                        ig, pg, free = ringA.take()
                        kg = mm(pg[:, :], wa[:, g0 + 128 * f:g0 + 128 * f + 128], src, free, src_ready)
                        yield c, pe, [ringA]
                        iu, pu, free = ringA.take()
                        ku = mm(pu[:, :], wa[:, u0 + 128 * f:u0 + 128 * f + 128], src, free, src_ready)
                        if e >= 0:
                            st["xe", e % 2] = ku
                        h, was = hg[f], st.get(("hg", f))
                        yield c, ac, [kg]
                        ka = act(h, pg[:, :], ACT.Tanh, kg, was, scale=0.5)
                        yield c, dv, [ka]
                        k = stt(h, h, 1.0, pg[:, :], ALU.add, ALU.mult, ka, kg)
                        ringA.free(ig, k)
                        yield c, dv, [k, ku]
                        k = stt(h, h, 0.5, pu[:, :], ALU.mult, ALU.mult, k, ku)
                        ringA.free(iu, k)
                        yield c, pe, [k]
                        ka = st["hg", f] = down(e, f, h, k)
                yield c, dv, [ka]
                k = tt(dv, rB, acc[:, :], x, ALU.add, ka, ready, st.get(("x2", c - 1)))
                st["acc_read"] = st["x1_read", c] = k
                yield c, pe, [K(c >= 2, "x2_read", c - 2)]
                last = lambda xc, rstd, w: tt(dv, x2[c % 2], xc, rstd, ALU.mult, w, st.get(("x2_read", c - 2)))
                st["x2", c] = yield from layernorm(c, ringA, 1, rB, k, last, st.get(("x2", c - 1)))

        def fast_weights():
            for c in range(NC):
                x = x2[c % 2]
                yield c, pe, [("x2", c)]
                ready = st["x2", c]
                done = st.get("fw_done")

                def project(w, f, out, scale, bias, extra=None):
                    yield c, pe, [ringA, ready]
                    i, pb, free = ringA.take()
                    k = mm(pb[:, :], wb[:, w], x, free, ready)
                    yield c, ac, [k, done]
                    k1 = act(out, pb[:, :], f, k, done, half, scale=scale, bias=bias)
                    k2 = act(extra, pb[:, :], ACT.Square, k, done, scale=1.0, bias=bias) if extra is not None else None
                    ringA.free(i, k1, k2)
                    return k1, k2

                kq, kq2 = yield from project(WB["wq"], ACT.Identity, q_s, 1.0, ba[:, BA["bq"]], sqq)
                kk, kk2 = yield from project(WB["wk"], ACT.Identity, k_s, 1.0, ba[:, BA["bk"]], sqk)
                kw_, _ = yield from project(WB["ww"], ACT.Tanh, tw, 0.5, hb[:, 1:2])
                kr_, _ = yield from project(WB["wr"], ACT.Tanh, tq, 0.5, hb[:, 2:3])
                yield c, pe, [ringA, kq2, kk2]
                i, pb, free = ringA.take()
                for n, (s, w) in enumerate(((sqq, kq2), (sqk, kk2))):
                    for j in range(4):
                        a = 16 * (4 * n + j)
                        k = mm(pb[:, a:a + 16], s[:, 128 * j:128 * j + 128], kc[:, KC["heads"]], w, free)
                nm, y, t = (sq[:, 0, 128 * n:128 * n + 128] for n in range(3))
                yield c, dv, [k]
                k = ts(nm, pb[:, 0:128], 1e-24, None, ALU.max, None, k)
                ringA.free(i, k)
                yield c, dv, [k]
                k = yield from rsqrt(c, nm, y, t, k)
                wide = m2[:, :, :].rearrange("p a b -> p (a b)")
                yield c, dv, [k]
                yb = y.unsqueeze(2).to_broadcast([P, 128, 8])
                k = dv(lambda e, yb=yb, wide=wide: e.tensor_copy(wide.rearrange("p (h d) -> p h d", d=8), yb), 1.2, k, st.get("wide_read"))
                out = []
                for n, (s, w, d) in enumerate(((q_s, kq, qn), (k_s, kk, kw))):
                    yield c, pe, [ringA, k]
                    i, pb, free = ringA.take()
                    for j in range(4):
                        a = 128 * (4 * n + j)
                        k2 = mm(pb[:, 128 * j:128 * j + 128], wide[:, a:a + 128], ident, k, free)
                    st["wide_read"] = k2
                    yield c, dv, [k2]
                    out.append(tt(dv, d, s, pb[:, :], ALU.mult, k2, w, done))
                    ringA.free(i, out[-1])
                yield c, dv, [out[1], kw_]
                kn = stt(kw, tw, 1.0, kw, ALU.add, ALU.mult, kw_, out[1])
                acc, acc_free = bank[6], st.get("fw_acc")
                ahead = None
                for r in range(9):
                    nxt = None
                    if r < 8:
                        yield c, pe, [ringA]
                        i, pb, free = ringA.take()
                        v0 = WB["wv"].start + 128 * r
                        k = mm(pb[:, :], wb[:, v0:v0 + 128], x, free, ready)
                        pr = m1[:, r % 2, :]
                        yield c, dv, [k]
                        b1 = BA["bv"].start + r
                        k = stt(pr, pb[:, :], ba[:, b1:b1 + 1], kw, ALU.add, ALU.mult, k, kn)
                        ringA.free(i, k)
                        yield c, dv, [k]
                        k = red(Ar[:, r % 2, :], pr.rearrange("p (s t) -> p t s", s=NB), ALU.add, k, st.get(("Ar", r % 2)))
                        z = zr[r % 2]
                        yield c, po, [k]
                        k = tt(po, bt(z), bt(qn), Ar[:, r % 2, :].unsqueeze(1).to_broadcast([P, NB, W]), ALU.mult, k, out[0],
                               st.get(("zr", r % 2)))
                        st["Ar", r % 2] = k
                        nxt = (r, z, k)
                    if ahead is not None:
                        r0, z0_, k0 = ahead
                        yield c, pe, [k0]
                        p0 = WB["perm"].start + 128 * r0
                        ka = mm(acc[:, :], wb[:, p0:p0 + 128], z0_, k0, acc_free, st=(r0 == 0), sp_=(r0 == 7))
                        st["zr", r0 % 2] = ka
                    ahead = nxt
                yield c, dv, [ka, kr_]
                k = st["fw_acc"] = stt(tq, tq, 1.0, acc[:, :], ALU.add, ALU.mult, ka, kr_)
                yield c, pe, [ringA, k]
                i, pb, free = ringA.take()
                k = mm(pb[:, :], wb[:, WB["wo"]], tq, free, k)
                st["fw_done"] = k
                yield c, dv, [k]
                k = stt(rC, pb[:, :], ba[:, BA["bo"]], x, ALU.add, ALU.add, k, ready, st.get(("x", c - 1)))
                ringA.free(i, k)
                st["x2_read", c] = k
                last = lambda xc, rstd, w: tt(dv, Xr[:, c, :], xc, rstd, ALU.mult, w)
                k = st["x", c] = yield from layernorm(c, ringA, 2, rC, k, last, st.get(("x", c - 1)))
                dma(g_keep, keep_d[:, c, :], Xr[:, c, :], k)

        take_turns([recurrence(), first_norm(), experts(), fast_weights()], st)

        phase = [Tok(q, len(q.ops) - 1, q.clock) for q in (pe, dv, ac, po)]
        t_keep = Tok(g_keep, g_keep.n, sp.clock + 2.0)

        kT = big0[:, :].rearrange("p (r b s t) -> p r b s t", r=8, b=NB, s=2)
        V2 = big1[:, :].rearrange("p (b n) -> p b n", b=NB)
        z0 = po(lambda e: e.memset(big0[:, :], 0.0), 7.0, phase)
        z1 = po(lambda e: e.memset(big1[:, :], 0.0), 7.0, phase)
        rg = Ring(bank, [0, 1, 2, 3])
        for b in rg.readers:
            rg.readers[b] = phase
        L = {}
        units = [(l, c) for l in range(DEPTH) for c in range(NC)]
        tiles = [(u, i) for u in range(len(units)) for i in range(4)]
        NG, NU = len(tiles), len(units)
        t_vec = dma(g_vec, vec[:, :, :], vec_d)
        for c in range(NC):
            L["X", -1, c] = st["x", c]

        def load_qkv(l):
            L["wqkv", l] = dma(g_big[l % 2], wqkv[:, l % 2, :], wqkv_d[l], L.get(("qkv_read", l - 2)), phase)

        def load_rest(l):
            L["wo", l] = dma(g_wo, wo[:, :, :], wo_d[l], L.get(("wo_read", l - 1)))

        def load_ffn(l):
            w = L.get(("ffn_read", l - 1))
            dma(g_ffn, w1[:, :], w1_d[l], w)
            L["ffn", l] = dma(g_ffn, w2[:, :, :], w2_d[l], w)

        def load_tables(l):
            w = L.get(("tab_read", l - 1))
            dma(g_tab, tab[:, :, :, :], tab_d, w)
            k = dma(g_tab, qsb[:, :, :], qs_d[l], w)
            for n in range(4):
                L["tab", l] = tt(po, tab[:, n, :, :], tab[:, n, :, :], qsb[:, n, :].unsqueeze(1).to_broadcast([P, NC, DH]),
                                 ALU.mult, k)

        def shifted(rank, dst, c, kind, *after):
            v = Xr[:, c, :].rearrange("p (b t) -> p b t", b=NB)
            d = dst.rearrange("p (b t) -> p b t", b=NB)
            edge = zero if c == 0 else halo[:, kind, :]
            yield rank, ac, list(flat(after))
            a = [act(dst[0:64, :], Xr[0:64, c, :], ACT.Copy, *after)]
            yield rank, ac, []
            a.append(act(d[64:128, :, 1:W], v[64:128, :, 0:W - 1], ACT.Copy, *after))
            yield rank, ac, []
            a.append(act(d[64:128, :, 0], edge[64:128, :], ACT.Copy, *after, L.get(("halo", kind)), t_zero))
            yield rank, ac, [a[-1]]
            L["halo", kind] = act(halo[64:128, kind, :], v[64:128, :, W - 1], ACT.Copy, *after, a[-1])
            return a + [L["halo", kind]]

        def lane_x():
            for u, (l, c) in enumerate(units):
                rank = 4 * u - 4
                yield rank, ac, [("X", l - 1, c), K(u >= 2, "xs_read", u - 2)]
                L["xs", u] = yield from shifted(rank, xs[:, u % 2, :], c, 0, L["X", l - 1, c], L.get(("xs_read", u - 2)), phase)

        def lane_a():
            for g, (u, i) in enumerate(tiles):
                l, c = units[u]
                rank = g - 3
                if i == 0 and c == 0:
                    if l == 0:
                        load_qkv(0)
                        load_rest(0)
                        load_ffn(0)
                    load_tables(l)
                if i == 0 and c == 1 and l + 1 < DEPTH:
                    load_qkv(l + 1)
                xt = xs[:, u % 2, 128 * i:128 * i + 128]
                wl = wqkv[:, l % 2, :]
                prods = []
                for part in range(4):
                    isk, h8 = part // 2, part % 2
                    col = INNER * isk + 512 * h8
                    yield rank, pe, [rg, ("xs", u), ("wqkv", l)]
                    ib, pb, free = rg.take()
                    k = mm(pb[:, :], xt, wl[:, col:col + 512], free, L["xs", u], L["wqkv", l])
                    s3 = part % 2
                    yield rank, ac, [k, K(4 * g + part >= 2, "sq", 4 * g + part - 2)]
                    ks = act(sq[:, s3, :], pb[:, :], ACT.Square, k, L.get(("sq", 4 * g + part - 2)))
                    ct, sn = tab[:, 2 * isk, c, :], tab[:, 2 * isk + 1, c, :]
                    o1 = m1[:, part, :].rearrange("p (h d) -> p h d", d=DH)
                    o2 = m2[:, s3, :].rearrange("p (h d) -> p h d", d=DH)
                    pv = pb[:, :].rearrange("p (h d) -> p h d", d=DH)
                    yield rank, dv, [ks, ("tab", l), K(g, "m1", g - 1, part)]
                    k1 = tt(dv, o1, pv, ct.unsqueeze(1).to_broadcast([P, 8, DH]), ALU.mult, k, ks, L["tab", l],
                            L.get(("m1", g - 1, part)))
                    yield rank, dv, [L.get(("m2", s3))]
                    k2 = tt(dv, o2[:, :, 0:32], pv[:, :, 32:64], sn[:, 0:32].unsqueeze(1).to_broadcast([P, 8, 32]), ALU.mult,
                            L.get(("m2", s3)))
                    k2 = tt(dv, o2[:, :, 32:64], pv[:, :, 0:32], sn[:, 32:64].unsqueeze(1).to_broadcast([P, 8, 32]), ALU.mult)
                    rg.free(ib, ks, k2)
                    L["tab_read", l] = k2
                    yield rank, dv, [K(g, "rot", g - 1)]
                    kr = red(ss[:, g % 2, 8 * part:8 * part + 8], sq[:, s3, :].rearrange("p (h d) -> p h d", d=DH), ALU.add, ks,
                             L.get(("ss", g % 2)))
                    L["sq", 4 * g + part] = kr
                    yield rank, po, [k2]
                    ka = tt(po, m1[:, part, :], m1[:, part, :], m2[:, s3, :], ALU.add, k1, k2)
                    L["m2", s3] = ka
                    prods.append(ka)
                L["prods", g] = (kr, prods)
                for par in range(2):
                    yield rank, pe, [rg]
                    ib, pb, free = rg.take()
                    col = 2 * INNER + 512 * par
                    k = mm(pb[:, :], xt, wl[:, col:col + 512], free)
                    yield rank, ac, [k, K(g, "v", g - 1)]
                    kv = act(vst[:, par, :], pb[:, :], ACT.Copy, k, L.get(("v", g - 1)))
                    rg.free(ib, kv)
                    rows = 64 * par + 32 * (c % 2)
                    yield rank, sp, [kv, K(g >= 4, "av", g - 4)]
                    for b in range(4):
                        kd = dma(g_v[g % 4], V2[rows:rows + 32, 4 * i + b, :], vst[32 * b:32 * b + 32, par, :], kv, z1,
                                 L.get(("av", g - 4)))
                L["v", g] = kd
                if i == 3:
                    L["xs_read", u] = k
                L["qkv_read", l] = k

        def lane_n():
            for g in range(NG):
                rank = g - 2.5
                yield rank, dv, [("prods", g), K(g >= 2, "rot", g - 2)]
                kr, prods = L["prods", g]
                nm, y, t = (nw[:, g % 2, n, 0:32] for n in range(3))
                k = ts(nm, ss[:, g % 2, :], 1e-24, None, ALU.max, None, kr, L.get(("nw", g % 2)))
                L["ss", g % 2] = k
                yield rank, dv, [k]
                k = yield from rsqrt(rank, nm, y, t, k)
                ready = []
                for part, ka in enumerate(prods):
                    o1 = m1[:, part, :].rearrange("p (h d) -> p h d", d=DH)
                    rb = y[:, 8 * part:8 * part + 8].unsqueeze(2).to_broadcast([P, 8, DH])
                    yield rank, po, [k, ka]
                    ready.append(tt(po, o1, o1, rb, ALU.mult, k, ka))
                    L["rot", g, part] = ready[-1]
                L["nw", g % 2] = ready[-1]
                L["rot", g] = ready

        def lane_b():
            for g, (u, i) in enumerate(tiles):
                l, c = units[u]
                rank = g - 2
                done = []
                for part in range(4):
                    isk, h8 = part // 2, part % 2
                    yield rank, pe, [rg, ("rot", g, part)]
                    ib, pb, free = rg.take()
                    for j in range(4):
                        k = tr(pb[:, 128 * j:128 * j + 128], m1[:, part, 128 * j:128 * j + 128], free, L["rot", g, part])
                    L["m1", g, part] = k
                    if isk:
                        d = kT[:, 4 * h8:4 * h8 + 4, 4 * i:4 * i + 4, c % 2, :]
                        yield rank, ac, [k, z0, K(g >= 4, "sim", g - 4)]
                        for j in range(4):
                            a = act(d[:, j], pb[:, 128 * j:128 * j + 128].rearrange("p (b t) -> p b t", b=4), ACT.Copy, k, z0,
                                    L.get(("sim", g - 4)))
                    else:
                        yield rank, ac, [k, K(g >= 2, "sim", g - 2)]
                        a = act(qT[:, g % 2, 4 * h8:4 * h8 + 4, :], pb[:, :].rearrange("p (r t) -> p r t", r=4), ACT.Copy, k,
                                L.get(("sim", g - 2)))
                    rg.free(ib, a)
                    done.append(a)
                L["T", g] = done

        def lane_c():
            for g, (u, i) in enumerate(tiles):
                l, c = units[u]
                rank = g - 1
                msk = kc[:, KC["mask"]].rearrange("p (v k) -> p v k", v=3)[:, 0 if c == 0 else 1 + c % 2, :]
                s = g % 2
                Sv = S[:, s, :].rearrange("p (r q k) -> p q r k", q=2, r=8)
                S16 = S[:, s, :].rearrange("p (h k) -> p h k", h=16)
                yield rank, pe, [("T", g), K(g, "masked", g - 1)]
                for r in range(8):
                    for par in range(2):
                        rows = slice(64 * par, 64 * par + 64)
                        for b in range(4):
                            k = mm(bank[4 + par][32 * b:32 * b + 32, 64 * r:64 * r + 64], qT[rows, s, r, 32 * b:32 * b + 32],
                                   kT[rows, r, 4 * i + b, :, :].rearrange("p s t -> p (s t)"), L["T", g],
                                   L.get(("masked", g - 1)), z0)
                L["sim", g] = k
                ka = []
                for par in range(2):
                    pv = bank[4 + par][:, :].rearrange("p (r k) -> p r k", r=8)
                    yield rank, dv, [k, K(g >= 2, "S", g - 2)]
                    ka.append(tt(dv, Sv[:, par], pv, msk.unsqueeze(1).to_broadcast([P, 8, 64]), ALU.add, k,
                                 L.get(("S", g - 2)), phase))
                L["masked", g] = ka
                yield rank, dv, ka
                k = red(mx[:, s, 0, :], S16, ALU.max, ka)
                yield rank, po, [k]
                k = tt(po, S16, S16, mx[:, s, 0, :].unsqueeze(2).to_broadcast([P, 16, 64]), ALU.subtract, k)
                yield rank, ac, [k]
                kx = act(S[:, s, :], S[:, s, :], ACT.Exp, k)
                L["exp", g] = kx
                yield rank, dv, [kx]
                k = red(mx[:, s, 1, :], S16, ALU.add, kx)
                L["summed", g] = k
                yield rank, dv, [k]
                L["sum", g] = dv(lambda e, s=s: e.reciprocal(rs[:, s, 0, :], mx[:, s, 1, :]), 0.2, k, L.get(("On", g - 2)))

        def lane_p():
            for g in range(NG):
                rank = g - 0.5
                ko = []
                for h in range(2):
                    yield rank, pe, [rg, ("exp", g)]
                    ib, pb, free = rg.take()
                    for j in range(4):
                        r = 4 * h + j
                        k = tr(pb[:, 128 * j:128 * j + 128], S[:, g % 2, 128 * r:128 * r + 128], free, L["exp", g])
                    yield rank, ac, [k, K(g, "av", g - 1)]
                    ko.append(act(P2[:, 4 * h:4 * h + 4, :], pb[:, :].rearrange("p (r t) -> p r t", r=4), ACT.Copy, k,
                                  L.get(("av", g - 1))))
                    rg.free(ib, ko[-1])
                yield rank, dv, [("summed", g)]
                L["S", g] = [k, L["summed", g]]
                L["P2", g] = ko

        def lane_d():
            for g, (u, i) in enumerate(tiles):
                s = g % 2
                ko = []
                yield g, pe, [("P2", g), ("v", g), K(g, "On", g - 1)]
                for r in range(8):
                    for par in range(2):
                        rows = slice(64 * par, 64 * par + 64)
                        for b in range(4):
                            k = mm(bank[6 + par][32 * b:32 * b + 32, 64 * r:64 * r + 64], P2[rows, r, 32 * b:32 * b + 32],
                                   V2[rows, 4 * i + b, 64 * r:64 * r + 64], L["P2", g], L["v", g], L.get(("On", g - 1)), z1)
                L["av", g] = k
                for par in range(2):
                    yield g, dv, [k, ("sum", g), K(g, "OnT", g - 1)]
                    o = On[:, 0, :].rearrange("p (r q d) -> p r q d", q=2, d=DH)[:, :, par, :]
                    rb = rs[:, s, 0, :].rearrange("p (r q) -> p q r", q=2)[:, par].unsqueeze(2).to_broadcast([P, 8, DH])
                    ko.append(tt(dv, o, bank[6 + par][:, :].rearrange("p (r d) -> p r d", d=DH), rb, ALU.mult, k, L["sum", g],
                                 L.get(("OnT", g - 1))))
                L["On", g] = ko

        def lane_e():
            for g in range(NG):
                ko = []
                rank = g + 0.5
                for h8 in range(2):
                    yield rank, pe, [rg, ("On", g)]
                    ib, pb, free = rg.take()
                    for j in range(4):
                        r = 4 * h8 + j
                        k = tr(pb[:, 128 * j:128 * j + 128], On[:, 0, 128 * r:128 * r + 128], free, L["On", g])
                    yield rank, ac, [k, K(g >= 2, "OT_read", g - 2)]
                    a = act(OT[:, g % 2, 4 * h8:4 * h8 + 4, :], pb[:, :].rearrange("p (r t) -> p r t", r=4), ACT.Copy, k,
                            L.get(("OT_read", g - 2)))
                    rg.free(ib, a)
                    ko.append(a)
                L["OnT", g] = k
                L["OT", g] = ko

        def lane_w():
            for g, (u, i) in enumerate(tiles):
                l, c = units[u]
                rank = g + 1
                yield rank, pe, [rg, ("OT", g), ("wo", l)]
                ib, pb, free = rg.take()
                for r in range(8):
                    k = mm(pb[:, 0:128], wo[:, r, :], OT[:, g % 2, r, :], free, L["OT", g], L["wo", l], st=(r == 0),
                           sp_=(r == 7))
                L["OT_read", g] = k
                L["wo_read", l] = k
                if i == 3 and c == NC - 1 and l + 1 < DEPTH:
                    load_rest(l + 1)
                xv = Xr[:, c, 128 * i:128 * i + 128]
                yield rank, dv, [k]
                k = tt(dv, xv, pb[:, 0:128], xv, ALU.add, k, L["xs", u], L["X", l - 1, c])
                rg.free(ib, k)
                L["res", g] = k

        def lane_f():
            for u, (l, c) in enumerate(units):
                rank = 4 * u + 5
                v = lambda n, rows=P, l=l: vec[0:rows, l, n:n + 1]
                yield rank, ac, [("res", 4 * u + i) for i in range(4)]
                ready = [L["res", 4 * u + i] for i in range(4)]
                a = yield from shifted(rank, x2s[:, :], c, 1, ready, L.get("x2s_read"))

                def last(xc, rstd, w):
                    return tt(dv, xn[:, :], xc, rstd, ALU.mult, w, L.get("xn_read"))

                k = yield from layernorm(rank, rg, 0, x2s[:, :], a, last, L.get("ln"))
                L["x2s_read"] = L["ln"] = k
                yield rank, ac, [k]
                kn = act(xn[:, :], xn[:, :], ACT.Identity, k, t_vec, scale=v(7), bias=v(8))
                kgs = []
                for f, rows in enumerate(FB):
                    yield rank + 1, pe, [rg, kn, ("ffn", l)]
                    ig, pg, free = rg.take()
                    kg = mm(pg[0:rows, :], w1[:, DI + 128 * f:DI + 128 * f + rows], xn[:, :], free, kn, L["ffn", l])
                    yield rank + 1, ac, [kg]
                    kgs.append(act(gg[0:rows, f, :], pg[0:rows, :], ACT.Gelu, kg, L.get(("gg", f)), bias=v(3 + f, rows)))
                    rg.free(ig, kgs[-1])
                kh = []
                for f, rows in enumerate(FB):
                    yield rank + 1, pe, [rg]
                    ia, pa, free = rg.take()
                    ka = mm(pa[0:rows, :], w1[:, 128 * f:128 * f + rows], xn[:, :], free)
                    yield rank + 1, dv, [ka, kgs[f], L.get("hh_read")]
                    k = stt(hh[0:rows, f, :], pa[0:rows, :], v(f, rows), gg[0:rows, f, :], ALU.add, ALU.mult, ka, kgs[f],
                            L.get("hh_read"))
                    L["gg", f] = k
                    rg.free(ia, k)
                    kh.append(k)
                L["xn_read"] = ka
                yield rank + 2, pe, [rg, *kh]
                ib, pb, free = rg.take()
                for f, rows in enumerate(FB):
                    k = mm(pb[:, :], w2[0:rows, f, :], hh[0:rows, f, :], free, kh, st=(f == 0), sp_=(f == 2))
                L["hh_read"] = L["ffn_read", l] = k
                if c == NC - 1 and l + 1 < DEPTH:
                    load_ffn(l + 1)
                yield rank + 2, dv, [k]
                k = stt(Xr[:, c, :], pb[:, :], v(6), Xr[:, c, :], ALU.add, ALU.add, k, a, ready)
                rg.free(ib, k)
                L["X", l, c] = k
                if l == DEPTH - 1:
                    kd = dma(g_back[c % 2], back[:, :], keep_d[:, c, :], t_keep, L.get("back"))
                    yield rank + 2, dv, [k, kd]
                    k = tt(dv, Xr[:, c, :], Xr[:, c, :], back[:, :], ALU.add, k, kd)
                    L["back"] = k
                    end = lambda xc, rstd, w, c=c: tt(dv, Xr[:, c, :], xc, rstd, ALU.mult, w)
                    k = yield from layernorm(rank + 2, rg, 0, Xr[:, c, :], k, end, L["ln"])
                    L["ln"] = k
                    dma(g_out, out_d[:, c, :], Xr[:, c, :], k)

        take_turns([lane_d(), lane_p(), lane_c(), lane_b(), lane_n(), lane_a(), lane_x(), lane_e(), lane_w(), lane_f()], L)
        sp(lambda e: None, 0.0, Tok(g_out, g_out.n, 0.0), Tok(g_keep, g_keep.n, 0.0))

        value = count_up([pe, dv, ac, po, sp])
        block = ctx.enter_context(nc.Block())

        def play_dma(q, eng):
            seen = {}
            for fn, after in q.ops:
                for t in flat(after):
                    v = value[(t.q, t.at)] if isinstance(t.q, Queue) else t.at
                    if seen.get(t.q, 0) < v:
                        eng.wait_ge(t.q.sem, v)
                        seen[t.q] = v
                fn(eng)

        @block.sync
        def _(eng):
            play_dma(sp, eng)

        @block.tensor
        def _(eng):
            play(pe, eng, value)

        @block.vector
        def _(eng):
            play(dv, eng, value)

        @block.scalar
        def _(eng):
            play(ac, eng, value)

        @block.gpsimd
        def _(eng):
            play(po, eng, value)


def shape_constants():
    f = np.float32
    kc, perm = np.zeros((P, KC_N), f), np.zeros((P, 8 * P), f)
    kc[:, KC["ident"]] = np.eye(P, dtype=f)
    kc[:, KC["center"]] = np.eye(P, dtype=f) - f(1.0 / P)
    n = np.arange(P)
    for r in range(8):
        m = np.zeros((P, P), f)
        m[n, 8 * (n // 8) + (n % 8 + r) % 8] = 0.25
        perm[:, P * r:P * r + P] = m
    kc[n, KC["heads"].start + n // 8] = 1.0
    kc[:, KC["mean"]] = 1.0 / P
    kc[:, KC["rank"]] = np.arange(8, 0, -1)
    low = f(-np.finfo(f).max)
    a, b = (n % W)[:, None], np.arange(W)[None, :]
    cur, prev = np.where(b <= a, f(0), low), np.where(b >= a, f(0), low)
    none = np.full((P, W), low, f)
    kc[:, KC["mask"]] = np.concatenate([cur, none, cur, prev, prev, cur], 1)
    half = np.arange(0, DH, 2, dtype=f)
    inv = (f(1.0) / np.power(f(10000.0), half / f(DH))).astype(f)
    t = np.arange(NT, dtype=f)
    fr = t[:, None] * inv[None, :]
    fr = np.concatenate([fr, fr], -1).astype(np.float64)
    base = ((half + f(0.4 * DH)) / f(1.4 * DH)).astype(f)
    power = (t - f(NT // 2)) / f(W // 2)
    sc = np.power(base[None, :].astype(np.float64), power[:, None].astype(np.float64))
    sc = np.concatenate([sc, sc], -1)
    sign = np.concatenate([-np.ones(DH // 2), np.ones(DH // 2)])
    tabs = np.stack([8.0 * np.cos(fr) * sc, 8.0 * np.sin(fr) * sc * sign, np.cos(fr) / sc, np.sin(fr) / sc * sign])
    tabs = tabs.reshape(4, NC, W, DH).transpose(2, 0, 1, 3)
    return kc, perm, np.tile(tabs, (4, 1, 1, 1)).astype(f)


def kernel(**inputs):
    import concourse.bacc as bacc
    from concourse.bass_utils import run_bass_kernel_spmd

    a = {k: np.asarray(v) for k, v in inputs.items()}
    f = np.float32
    kc, perm, tabs = shape_constants()
    rot = lambda w, r: np.concatenate([np.roll(w[8 * h:8 * h + 8], -r, 0) for h in range(16)])
    A = lambda n: a["L1_attn_" + n]
    down = lambda w: w.T.reshape(2, 128, 128).transpose(1, 0, 2).reshape(128, 256)
    wa = np.zeros((P, WA_N), f)
    put = {"ws": a["L0_attn_W_state"].T, "wg": a["L0_attn_W_gate"].T, "router": a["L0_ffn_gate_w"].T,
           "sg": a["L0_ffn_shared_gate"].T, "su": a["L0_ffn_shared_up"].T, "sd": down(a["L0_ffn_shared_down"]),
           "eg": a["L0_ffn_r_gate"].transpose(2, 0, 1).reshape(128, -1),
           "eu": a["L0_ffn_r_up"].transpose(2, 0, 1).reshape(128, -1),
           "ed": np.concatenate([down(w) for w in a["L0_ffn_r_down"]], 1),
           "wq": A("Wq_w").T, "wk": A("Wk_w").T, "ww": np.repeat(A("Ww_w").T, 8, 1), "wr": np.repeat(A("Wr_w").T, 8, 1),
           "wv": np.concatenate([rot(A("Wv_w"), r).T for r in range(8)], 1), "wo": A("Wo_w").T}
    wb = np.zeros((P, WB_N), f)
    put["perm"] = perm
    for n, w in put.items():
        if n in WA:
            wa[:, WA[n]] = w
        else:
            wb[:, WB[n]] = w
    ba = np.zeros((P, BA_N), f)
    put = {"bs": a["L0_attn_b_state"][:, None], "bg": a["L0_attn_b_gate"][:, None], "bq": A("Wq_b")[:, None],
           "bk": A("Wk_b")[:, None], "bw": np.repeat(A("Ww_b"), 8)[:, None], "br": np.repeat(A("Wr_b"), 8)[:, None],
           "bv": np.stack([rot(A("Wv_b"), r) for r in range(8)], 1), "bo": A("Wo_b")[:, None]}
    for n, w in put.items():
        ba[:, BA[n]] = w
    B = lambda n: a["L1_ffn_" + n]
    swap = lambda s: np.concatenate([s[:, 32:], s[:, :32]], 1)
    qs = np.stack([B("q_scale"), swap(B("q_scale")), B("k_scale"), swap(B("k_scale"))], 1)
    qs = np.ascontiguousarray(np.broadcast_to(qs[:, None], (DEPTH, P, 4, DH)))
    wv = B("Wqkv")[:, :, 2 * INNER:].reshape(DEPTH, C, 8, 2, DH).transpose(0, 1, 3, 2, 4).reshape(DEPTH, C, INNER)
    wqkv = np.concatenate([B("Wqkv")[:, :, :2 * INNER], wv], 2)
    w2 = np.zeros((DEPTH, 3 * P, C), f)
    w2[:, :DI] = B("W2")
    vec = np.zeros((P, DEPTH, 9), f)
    for l in range(DEPTH):
        for n in range(2):
            for m, rows in enumerate(FB):
                vec[:rows, l, 3 * n + m] = B("b1")[l, DI * n + 128 * m:DI * n + 128 * m + rows]
        vec[:, l, 6], vec[:, l, 7], vec[:, l, 8] = B("b2")[l], B("ln_g")[l], B("ln_b")[l]
    arrays = {
        "x": a["L0_attn_x"].reshape(NB, NC, W, C).transpose(3, 1, 0, 2).reshape(C, NC, N),
        "kc": kc, "wa": wa, "wb": wb, "ba": ba, "tab": tabs, "qs": qs, "wqkv": wqkv,
        "wo": B("Wo").reshape(DEPTH, 8, 128, C).transpose(0, 2, 1, 3), "w1": B("W1"),
        "w2": w2.reshape(DEPTH, 3, P, C).transpose(0, 2, 1, 3), "vec": vec,
    }
    nc = bacc.Bacc("TRN2", target_bir_lowering=False, num_devices=1)
    ins, args = {}, []
    for n, v in arrays.items():
        v = np.ascontiguousarray(v)
        ins["in_" + n] = v
        args.append(nc.dram_tensor("in_" + n, v.shape, F32, kind="ExternalInput").ap())
    out = nc.dram_tensor("out", (C, NC, N), F32, kind="ExternalOutput").ap()
    keep = nc.dram_tensor("keep", (C, NC, N), F32, kind="Internal").ap()
    program(nc, *args, out, keep)
    r = run_bass_kernel_spmd(nc, [ins], core_ids=[0])
    y = np.asarray(r.results[0]["out"])
    return np.ascontiguousarray(y.reshape(C, NC, NB, W).transpose(2, 1, 3, 0)).reshape(NB, NT, C)
```

```python
from contextlib import ExitStack

import numpy as np
import concourse.bass as bass
from concourse import mybir

F32 = mybir.dt.float32
F32R = mybir.dt.float32r
I32 = mybir.dt.int32
ALU = mybir.AluOpType
ACT = mybir.ActivationFunctionType
X_AX = mybir.AxisListType.X

P = 128
NB, NT, C = 16, 256, 128
NC, W = 8, 32
N = NB * W
DEPTH, HEADS, DH = 6, 16, 64
INNER = HEADS * DH
DI = 341
FB = [128, 128, 85]
E = 8
MAGIC = 1597463007.0

RANK = {'x': -4.5, 'a': -3, 'v': -1.5, 'n': -2.375, 'b': -2.625, 'c': -0.625, 'p': -0.5, 'e': 0.0, 'w': 0.75, 'f': 6.75, 'f1': 2.0, 'f2': 1.875, 'soon': 0.15, 'A1': -1.5, 'Ar': -0.125, 'As': 1, 'Ae': -0.375, 'Af': 0.5, 'soonA': -1.6}


class Tok:
    __slots__ = ("q", "at", "t")

    def __init__(self, q, at, t):
        self.q, self.at, self.t = q, at, t


class Queue:

    def __init__(self, sem):
        self.sem, self.ops, self.clock = sem, [], 0.0

    def __call__(self, fn, cost, *after):
        start = max([self.clock] + [t.t + (0.13 if t.q is self else 0.2) for t in flat(after)])
        self.clock = start + cost
        tok = Tok(self, len(self.ops), self.clock)
        self.ops.append((fn, after))
        return tok


class Dmas:

    def __init__(self, sem):
        self.sem, self.n = sem, 0


def flat(after):
    for t in after:
        if isinstance(t, (list, tuple)):
            yield from flat(t)
        elif t is not None:
            yield t


def count_up(queues):
    named = {q: set() for q in queues}
    for q in queues:
        for _, after in q.ops:
            for t in flat(after):
                if t.q in named:
                    named[t.q].add(t.at)
    value = {}
    for q in queues:
        for n, at in enumerate(sorted(named[q])):
            value[(q, at)] = n + 1
    return value


def play(q, eng, value):
    seen = {}
    for i, (fn, after) in enumerate(q.ops):
        need = {}
        for t in flat(after):
            v = value[(t.q, t.at)] if isinstance(t.q, Queue) else t.at
            need[t.q] = max(v, need.get(t.q, 0))
        for src, v in need.items():
            if seen.get(src, 0) < v:
                eng.wait_ge(src.sem, v)
                seen[src] = v
        ins = fn(eng)
        if (q, i) in value:
            ins.then_inc(q.sem, 1)


def take_turns(lanes, known, soon_by):
    ahead = {}
    lanes = list(lanes)
    for g in list(lanes):
        ahead[g] = next(g, None)
    while True:
        best = None
        for g in lanes:
            if ahead[g] is None:
                continue
            rank, q, needs = ahead[g]
            t = q.clock
            for n in needs:
                if isinstance(n, Ring):
                    n = n.soonest()
                elif isinstance(n, tuple):
                    n = known.get(n, False)
                if n is False:
                    t = None
                    break
                for x in flat([n]):
                    t = max(t, x.t + (0.13 if x.q is q else 0.2))
            if t is not None and (best is None or (t, rank) < best[:2]):
                best = (t, rank, g)
        if best is None:
            assert all(ahead[g] is None for g in lanes), [ahead[g] for g in lanes]
            return
        soon = best[0] + soon_by
        for g in lanes:
            if ahead[g] is None or g is best[2]:
                continue
            rank, q, needs = ahead[g]
            if rank >= best[1]:
                continue
            t = q.clock
            for n in needs:
                if isinstance(n, Ring):
                    n = n.soonest()
                elif isinstance(n, tuple):
                    n = known.get(n, False)
                if n is False:
                    t = None
                    break
                for x in flat([n]):
                    t = max(t, x.t + (0.13 if x.q is q else 0.2))
            if t is not None and t <= soon:
                best = (t, rank, g)
        ahead[best[2]] = next(best[2], None)


def ranked(name, lane):
    for rank, q, needs in lane:
        yield rank + RANK[name], q, needs


class Ring:

    def __init__(self, bank, banks):
        self.bank, self.free_now, self.readers = bank, list(banks), {b: [] for b in banks}

    def when(self, b):
        return max([t.t for t in flat(self.readers[b])], default=0.0)

    def soonest(self):
        if not self.free_now:
            return False
        return self.readers[min(self.free_now, key=self.when)]

    def take(self):
        b = min(self.free_now, key=self.when)
        self.free_now.remove(b)
        return b, self.bank[b], self.readers[b]

    def free(self, b, *readers):
        self.readers[b] = list(readers)
        self.free_now.append(b)


def columns(sizes):
    at, out = 0, {}
    for name, n in sizes:
        out[name] = slice(at, at + n)
        at += n
    return out, at


KC, KC_N = columns([("ident", 128), ("center", 128), ("heads", 16), ("mean", 1), ("rank", 8), ("mask", 3 * 64)])
WA, WA_N = columns([("ws", 128), ("wg", 128), ("router", 8), ("sg", 256), ("su", 256), ("sd", 256),
                    ("eg", E * 256), ("eu", E * 256), ("ed", E * 256)])
WB, WB_N = columns([("wq", 128), ("wk", 128), ("ww", 128), ("wr", 128), ("wv", 8 * 128), ("wo", 128), ("perm", 8 * 128)])
BA, BA_N = columns([("bs", 1), ("bg", 1), ("bq", 1), ("bk", 1), ("bw", 1), ("br", 1), ("bv", 8), ("bo", 1)])


def program(nc, x_d, kc_d, wa_d, wb_d, ba_d, tab_d, qs_d, wqkv_d, wo_d, w1_d, w2_d, vec_d, out_d, keep_d):
    with ExitStack() as ctx:
        def sb(name, shape, dt=F32):
            return ctx.enter_context(nc.sbuf_tensor(name, shape, dt))

        def sem(name):
            return ctx.enter_context(nc.semaphore(name))

        bank = [ctx.enter_context(nc.psum_tensor(f"bank{i}", [P, 512], F32)) for i in range(8)]
        pe, dv, ac, po = (Queue(sem(n)) for n in ("s_pe", "s_dv", "s_ac", "s_po"))
        sp = Queue(sem("s_sp"))

        def size(ap):
            n = 1
            for d in ap.shape[1:]:
                n *= d
            return n

        def dma(group, out, in_, *after):
            group.n += 16
            k = sp(lambda e: e.dma_start(out, in_).then_inc(group.sem, 16) and None, 0.65, *after)
            return Tok(group, group.n, k.t + 2.0)

        def mm(out, l, r, *after, st=True, sp_=True):
            n, m = size(r), size(l)
            cost = 0.048 if m <= 64 else max(0.107, n * 2 * 2 / 2400)
            return pe(lambda e: e.matmul(out, l, r, start=st, stop=sp_), cost, *after)

        def mm3(out, l, r, *after):
            for n, (a, b) in enumerate(((0, 0), (1, 0), (0, 1))):
                k = pe(lambda e, a=a, b=b, n=n: e.matmul(out, l[a], r[b], start=n == 0, stop=n == 2), size(r[b]) / 2400, *after)
            return k

        def tr(out, in_, *after):
            return pe(lambda e: e.transpose(out, in_, kc[:, KC["ident"]]), 0.107, *after)

        def act(out, in_, f, *after, scale=1.0, bias=0.0):
            return ac(lambda e: e.activation(out, in_, f, scale=scale, bias=bias), 0.06 + size(out) / 1200, *after)

        def tt(q, out, a, b, op, *after):
            n = size(out)
            return q(lambda e: e.tensor_tensor(out, a, b, op), 0.066 + n / 960 if q is dv else 0.1 + 0.00175 * n if n > 512 else 0.1 + 0.0021 * n, *after)

        def stt(out, a, s, b, op0, op1, *after):
            return dv(lambda e: e.scalar_tensor_tensor(out, a, s, b, op0, op1), 0.1 + size(out) / 960, *after)

        def ts(out, a, s1, s2, op0, op1, *after):
            cost = 0.066 + size(out) / 960
            if op1 is None:
                return dv(lambda e: e.tensor_scalar(out, a, s1, None, op0), cost, *after)
            return dv(lambda e: e.tensor_scalar(out, a, s1, s2, op0, op1), cost, *after)

        def red(out, in_, op, *after):
            return dv(lambda e: e.tensor_reduce(out, in_, axis=X_AX, op=op), 0.066 + size(in_) / 960, *after)

        kc = sb("kc", [P, KC_N])
        ba = sb("ba", [P, BA_N])
        hb = sb("hb", [P, 3])
        Xr = sb("Xr", [P, NC, N])
        big0 = sb("big0", [P, 8192])
        big1 = sb("big1", [P, 8192])
        wqkv = sb("wqkv", [P, 2, 3 * INNER], F32R)
        stage = sb("stage", [P, 2, 512])
        wo = sb("wo", [P, 8, 128])
        ffn = sb("ffn", [P, 2 * DI + 3 * 128])
        w1, w2 = ffn[:, 0:2 * DI], ffn[:, 2 * DI:].rearrange("p (f n) -> p f n", f=3)
        vec = sb("vec", [P, DEPTH, 9])
        tab = sb("tab", [P, 2, 4, DH])
        qsb = sb("qsb", [P, 2, 4, DH])
        halo = sb("halo", [P, 2, NB])
        zero = sb("zero", [P, NB])
        xs = sb("xs", [P, 2, 2, N], F32R)
        sq = sb("sq", [P, 2, 512])
        m1 = sb("m1", [P, 4, 512])
        m2 = sb("m2", [P, 2, 512])
        ss = sb("ss", [P, 2, 32])
        nw = sb("nw", [P, 2, 3, 32])
        qT = sb("qT", [P, 2, 8, P])
        S = sb("S", [P, 2, 1024])
        On = sb("On", [P, 1, 1024])
        OT = sb("OT", [P, 2, 8, P])
        vst = sb("vst", [P, 2, 512])
        P2 = sb("P2", [P, 8, P])
        mx = sb("mx", [P, 2, 2, 16])
        rs = sb("rs", [P, 2, 2, 16])
        x2s = sb("x2s", [P, N])
        lc = sb("lc", [P, N])
        ls = sb("ls", [P, N])
        lv = sb("lv", [P, 3, 4])
        lr = sb("lr", [P, 3, 3, 4])
        xn = sb("xn", [P, N])
        gg = sb("gg", [P, 3, N])
        hh = sb("hh", [P, 3, N])


        g_kc, g_ws, g_wa, g_vec, g_keep, g_out = (Dmas(sem(n)) for n in ("d_kc", "d_ws", "d_wa", "d_vec", "d_keep", "d_out"))
        g_x = [Dmas(sem(f"d_x{i}")) for i in range(2)]
        g_back = [Dmas(sem(f"d_back{i}")) for i in range(2)]
        g_big = [Dmas(sem(f"d_wqkv{i}")) for i in range(2)]
        g_v = [Dmas(sem(f"d_v{i}")) for i in range(4)]
        g_wo, g_ffn = Dmas(sem("d_wo")), Dmas(sem("d_ffn"))
        g_tab = [Dmas(sem(f"d_tab{i}")) for i in range(2)]
        g_qs = [Dmas(sem(f"d_qs{i}")) for i in range(2)]

        wa = big1
        xin = [big0[:, 512 * i:512 * (i + 1)] for i in range(2)]
        wb = {"wv": wo[:, :, :].rearrange("p a b -> p (a b)"), "perm": ffn[:, 0:1024],
              "wo": tab[:, 0, 0:2, :].rearrange("p a b -> p (a b)")}
        for n, name in enumerate(("wq", "wk", "ww", "wr")):
            wb[name] = qsb[:, n // 2, 2 * (n % 2):2 * (n % 2) + 2, :].rearrange("p a b -> p (a b)")
        back = stage[:, 0, :]
        first = slice(0, 256)
        t_ws = dma(g_ws, wa[:, first], wa_d[:, first])

        t_x0 = dma(g_x[0], xin[0], x_d[:, 0, :])
        dma(g_kc, ba[:, :], ba_d)
        t_kc = dma(g_kc, kc[:, :], kc_d)
        dma(g_wa, wa[:, 256:WA_N], wa_d[:, 256:WA_N])
        for name, ap in wb.items():
            t_wa = dma(g_wa, ap, wb_d[:, WB[name]])

        def rsqrt(rank, a, y, t, *after):
            n = size(a) / 960 + 0.066
            k = dv(lambda e: e.tensor_scalar(t.bitcast(I32), a.bitcast(I32), 1, None, ALU.logical_shift_right), n, *after)
            yield rank, dv, [k]
            k = dv(lambda e: e.tensor_scalar(y.bitcast(I32), t.bitcast(I32), -1.0, MAGIC, ALU.mult, ALU.add), n, k)
            for _ in range(3):
                yield rank, dv, [k]
                k = tt(dv, t, y, y, ALU.mult, k)
                yield rank, dv, [k]
                k = stt(t, t, -0.5, a, ALU.mult, ALU.mult, k)
                yield rank, dv, [k]
                k = stt(y, t, 1.5, y, ALU.add, ALU.mult, k)
            return k

        LN = [(lc[:, :], ls[:, :]), (gg[:, 0, :], gg[:, 1, :]), (hh[:, 0, :], hh[:, 1, :])]

        def layernorm(rank, ring, b, src, src_ready, last, busy):
            bc, bs = LN[b]
            yield rank, pe, [ring, src_ready]
            i, pb, free = ring.take()
            k = mm(pb[:, :], kc[:, KC["center"]], src, free, src_ready, t_kc)
            yield rank, ac, [k, busy]
            a1 = act(bc, pb[:, :], ACT.Copy, k, busy)
            a2 = act(bs, pb[:, :], ACT.Square, k, busy)
            ring.free(i, a1, a2)
            yield rank, pe, [ring, a2]
            i, pb, free = ring.take()
            for j in range(4):
                k = mm(pb[:, j:j + 1], bs[:, 128 * j:128 * j + 128], kc[:, KC["mean"]], a2, free)
            yield rank, dv, [k]
            k = ts(lv[:, b, :], pb[:, 0:4], 1e-5, None, ALU.add, None, k)
            ring.free(i, k)
            yield rank, dv, [k]
            k = yield from rsqrt(rank, lv[:, b, :], lr[:, b, 0, :], lr[:, b, 1, :], k)
            yield rank, pe, [ring, k]
            i, pb, free = ring.take()
            for j in range(4):
                k2 = tr(pb[:, 128 * j:128 * j + 128], lr[:, b, 0, j:j + 1].to_broadcast([P, P]), k, free)
            yield rank, dv, [k2, a1]
            k = last(bc, pb[:, :], [k2, a1])
            ring.free(i, k)
            return k

        ringA = Ring(bank, range(8))
        V = lambda i: big0[:, 1024 + 512 * i:1536 + 512 * i]
        pP, tg, hist = V(0), V(1), [V(2), V(3)]
        x1, x2 = [V(4), V(5)], [V(6), V(7)]
        xe = [V(8), V(9)]
        hg = [V(10), V(11)]
        kw, qn, zr = V(12), V(13), [hh[:, 0, :], hh[:, 1, :]]
        rA, rB, rC = S[:, 0, 0:512], S[:, 0, 512:1024], S[:, 1, 0:512]
        q_s, k_s, tw, tq = OT[:, 0, 0:4, :].rearrange("p a b -> p (a b)"), OT[:, 0, 4:8, :].rearrange("p a b -> p (a b)"), vst[:, 0, :], vst[:, 1, :]
        sqq, sqk = On[:, 0, 0:512], On[:, 0, 512:1024]
        step_in = sb("step_in", [P, 2, NB])
        lg = sb("lg", [P, 4, 8])
        eqv = sb("eqv", [P, 4, 8])
        oh = sb("oh", [P, 4, 8])
        mxl = sb("mxl", [P, 3, 4])
        Ar = sb("Ar", [P, 2, W])
        bt = lambda ap: ap.rearrange("p (b t) -> p b t", b=NB)

        for n, name in enumerate(("bg", "bw", "br")):
            half = ts(hb[:, n:n + 1], ba[:, BA[name]], 0.5, None, ALU.mult, None, t_kc)
        t_zero = dv(lambda e: e.memset(zero[:, :], 0.0), 0.1)

        st = {}

        def K(when, *key):
            return key if when else None

        def recurrence():
            state = None
            for c in range(NC):
                x = xin[c % 2]
                yield c, sp, [K(c >= 2, "u1", c - 2)]
                t_in = dma(g_x[c % 2], x, x_d[:, c, :], st.get(("u1", c - 2))) if c else t_x0
                yield c, pe, [t_in, t_ws, ringA]
                i, pb, free = ringA.take()
                k = mm(pb[:, :], wa[:, WA["ws"]], x, free, t_in, t_ws)
                yield c, ac, [k]
                kp = act(pP, pb[:, :], ACT.Identity, k, st.get(("pP", c - 1)), t_kc, bias=ba[:, BA["bs"]])
                ringA.free(i, kp)
                yield c, pe, [ringA]
                i, pb, free = ringA.take()
                k = mm(pb[:, :], wa[:, WA["wg"]], x, free)
                yield c, ac, [k, K(c, "u0", c - 1)]
                kg = act(tg, pb[:, :], ACT.Tanh, k, half, st.get(("u0", c - 1)), scale=0.5, bias=hb[:, 0:1])
                ringA.free(i, kg)
                h = bt(hist[c % 2])
                busy = st.get(("u0", c - 2))
                for t in range(W):
                    if c == 0 and t == 0:
                        yield c, ac, [kp]
                        state = act(h[:, :, 0], bt(pP)[:, :, 0], ACT.Tanh, kp)
                        continue
                    prev = h[:, :, t - 1] if t else bt(hist[(c - 1) % 2])[:, :, W - 1]
                    yield -1, dv, [state, kp]
                    k = tt(dv, step_in[:, t % 2, :], bt(pP)[:, :, t], prev, ALU.add, state, kp)
                    yield -1, ac, [k]
                    state = act(h[:, :, t], step_in[:, t % 2, :], ACT.Tanh, k, busy)
                st["pP", c] = k
                st["hist", c] = state
                st["kg", c] = kg

        def first_norm():
            for c in range(NC):
                yield c, dv, [("hist", c)]
                k1 = stt(rA, tg, 1.0, hist[c % 2], ALU.add, ALU.mult, st["hist", c], st["kg", c], st.get(("x1", c - 1)))
                st["u0", c] = k1
                yield c, dv, [k1]
                k2 = stt(rA, rA, 0.5, xin[c % 2], ALU.mult, ALU.add, k1)
                st["u1", c] = k2
                yield c, dv, [K(c >= 2, "x1_read", c - 2)]
                last = lambda xc, rstd, w: tt(dv, x1[c % 2], xc, rstd, ALU.mult, w, st.get(("x1_read", c - 2)))
                st["x1", c] = yield from layernorm(c, ringA, 0, rA, k2, last, st.get(("x1", c - 1)))

        masks = [qT[:, i, 4 * j:4 * j + 4, :].rearrange("p a b -> p (a b)") for i in range(2) for j in range(2)]
        masks += [ap[:, 4 * j:4 * j + 4, :].rearrange("p a b -> p (a b)") for ap in (P2, OT[:, 1]) for j in range(2)]
        xp = sq[:, 1, :]
        hs, hf = hg, [x2s[:, :], xn[:, :]]
        hm = [m1[:, 3, :], gg[:, 2, :], hh[:, 2, :], m1[:, 2, :]]

        def router():
            for c in range(NC):
                x = x1[c % 2]
                yield c, pe, [("x1", c), ringA]
                ready = st["x1", c]
                i, pb, free = ringA.take()
                for j in range(4):
                    k = mm(pb[:, 8 * j:8 * j + 8], x[:, 128 * j:128 * j + 128], wa[:, WA["router"]], free, ready, t_wa)
                yield c, dv, [k]
                raw = pb[:, 0:32].rearrange("p (j e) -> p j e", e=8)
                k = dv(lambda e, raw=raw: e.tensor_copy(lg[:, :, :], raw), 0.1, k)
                ringA.free(i, k)
                yield c, dv, [k]
                k = red(mxl[:, 0, :], lg[:, :, :], ALU.max, k)
                yield c, ac, [k]
                kt = act(mxl[:, 1, :], mxl[:, 0, :], ACT.Tanh, k, st.get("p_read"), scale=0.5)
                mb = lambda n: mxl[:, n, :].unsqueeze(2).to_broadcast([P, 4, 8])
                yield c, dv, [kt]
                kt = ts(mxl[:, 1, :], mxl[:, 1, :], 0.5, 0.5, ALU.mult, ALU.add, kt)
                yield c, dv, [k]
                k = tt(dv, eqv[:, :, :], lg[:, :, :], mb(0), ALU.is_equal, k)
                yield c, dv, [k]
                k = tt(dv, eqv[:, :, :], eqv[:, :, :], kc[:, KC["rank"]].unsqueeze(1).to_broadcast([P, 4, 8]), ALU.mult, k)
                yield c, dv, [k]
                k = red(mxl[:, 2, :], eqv[:, :, :], ALU.max, k)
                yield c, dv, [k]
                chosen = tt(dv, oh[:, :, :], eqv[:, :, :], mb(2), ALU.is_equal, k, st.get("oh_read"))
                yield c, pe, [ringA, kt]
                i, pb, free = ringA.take()
                for j in range(4):
                    k = tr(pb[:, 128 * j:128 * j + 128], mxl[:, 1, j:j + 1].to_broadcast([P, P]), free, kt)
                st["p_read"] = k
                yield c, dv, [k, K(c, "xp_read", c - 1)]
                st["xp", c] = tt(dv, xp, x, pb[:, :], ALU.mult, k, ready, st.get(("xp_read", c - 1)))
                ringA.free(i, st["xp", c])
                for e in range(E):
                    yield c, pe, [ringA, chosen]
                    i, pb, free = ringA.take()
                    for j in range(4):
                        k = tr(pb[:, 128 * j:128 * j + 128], oh[:, j, e:e + 1].to_broadcast([P, P]), free, chosen)
                    st["oh_read"] = k
                    yield c, ac, [k, K(c, "mask_read", c - 1, e)]
                    st["mask", c, e] = act(masks[e], pb[:, :], ACT.Copy, k, st.get(("mask_read", c - 1, e)))
                    ringA.free(i, st["mask", c, e])

        def gated(rank, h, was, g, u):
            (ig, pg, kg), (iu, pu, ku) = g, u
            yield rank, ac, [kg, was]
            ka = act(h, pg[:, :], ACT.Tanh, kg, was, scale=0.5)
            yield rank, dv, [ka]
            k = stt(h, h, 1.0, pg[:, :], ALU.add, ALU.mult, ka, kg)
            ringA.free(ig, k)
            yield rank, dv, [k, ku]
            k = stt(h, h, 0.5, pu[:, :], ALU.mult, ALU.mult, k, ku)
            ringA.free(iu, k)
            return k

        def shared():
            for c in range(NC):
                for f in range(2):
                    got = []
                    for w in ("sg", "su"):
                        yield c, pe, [ringA, ("x1", c)]
                        i, pb, free = ringA.take()
                        w0 = WA[w].start + 128 * f
                        got.append((i, pb, mm(pb[:, :], wa[:, w0:w0 + 128], x1[c % 2], free, st["x1", c], t_wa)))
                    yield c, ac, [K(c, "hs_read", c - 1)]
                    st["hs", c, f] = yield from gated(c, hs[f], st.get(("hs_read", c - 1)), *got)

        def experts():
            n_hm = 0
            for c in range(NC):
                x, ready = x1[c % 2], st.get(("x1", c))
                got = []
                for e in range(E):
                    src = xe[e % 2]
                    yield c, dv, [("xp", c), ("mask", c, e)]
                    k = tt(dv, src, xp, masks[e], ALU.mult, st["xp", c], st["mask", c, e], st.get(("xe", e % 2)))
                    if e == E - 1:
                        st["xp_read", c] = k
                    for n in range(4):
                        if e == 0:
                            yield c, pe, [ringA, k]
                            got.append(list(ringA.take()))
                        elif n == 0:
                            yield c, pe, [k]
                        w0 = WA["eg" if n < 2 else "eu"].start + 256 * e + 128 * (n % 2)
                        got[n][2] = mm(got[n][1][:, :], wa[:, w0:w0 + 128], src, got[n][2] if e == 0 else None, k, st=(e == 0),
                                       sp_=(e == E - 1))
                    st["xe", e % 2] = got[3][2]
                kh = []
                for f in range(2):
                    kh.append((yield from gated(c, hf[f], st.get(("hf_read", f)), got[f], got[2 + f])))
                yield c, pe, [ringA, ("hs", c, 0), ("hs", c, 1)]
                ia, acc, free = ringA.take()
                for f in range(2):
                    w0 = WA["sd"].start + 128 * f
                    k = mm(acc[:, :], wa[:, w0:w0 + 128], hs[f], free, st["hs", c, f], st=(f == 0), sp_=False)
                st["hs_read", c] = k
                for e in range(E):
                    for f in range(2):
                        q, m = (dv, po)[f], hm[n_hm % 4]
                        yield c, q, [kh[f], st.get(("hm", n_hm % 4))]
                        k = tt(q, m, hf[f], masks[e], ALU.mult, kh[f], st["mask", c, e], st.get(("hm", n_hm % 4)))
                        st["hf_read", f] = k
                        if f == 0:
                            k0 = k
                        else:
                            st["mask_read", c, e] = [k0, k]
                        yield c, pe, [k]
                        w0 = WA["ed"].start + 256 * e + 128 * f
                        k = mm(acc[:, :], wa[:, w0:w0 + 128], m, k, st=False, sp_=(e == E - 1 and f == 1))
                        st["hm", n_hm % 4] = k
                        n_hm += 1
                yield c, dv, [k]
                k = tt(dv, rB, acc[:, :], x, ALU.add, k, st["x1", c], st.get(("x2", c - 1)))
                ringA.free(ia, k)
                st["x1_read", c] = k
                yield c, pe, [K(c >= 2, "x2_read", c - 2)]
                last = lambda xc, rstd, w: tt(dv, x2[c % 2], xc, rstd, ALU.mult, w, st.get(("x2_read", c - 2)))
                st["x2", c] = yield from layernorm(c, ringA, 1, rB, k, last, st.get(("x2", c - 1)))

        def fast_weights():
            for c in range(NC):
                x = x2[c % 2]
                yield c, pe, [("x2", c)]
                ready = st["x2", c]
                done = st.get("fw_done")

                def project(w, f, out, scale, bias, extra=None):
                    yield c, pe, [ringA, ready]
                    i, pb, free = ringA.take()
                    k = mm(pb[:, :], wb[w], x, free, ready)
                    yield c, ac, [k, done]
                    k1 = act(out, pb[:, :], f, k, done, half, scale=scale, bias=bias)
                    k2 = act(extra, pb[:, :], ACT.Square, k, done, scale=1.0, bias=bias) if extra is not None else None
                    ringA.free(i, k1, k2)
                    return k1, k2

                kq, kq2 = yield from project("wq", ACT.Identity, q_s, 1.0, ba[:, BA["bq"]], sqq)
                kk, kk2 = yield from project("wk", ACT.Identity, k_s, 1.0, ba[:, BA["bk"]], sqk)
                kw_, _ = yield from project("ww", ACT.Tanh, tw, 0.5, hb[:, 1:2])
                kr_, _ = yield from project("wr", ACT.Tanh, tq, 0.5, hb[:, 2:3])
                yield c, pe, [ringA, kq2, kk2]
                i, pb, free = ringA.take()
                for n, (s, w) in enumerate(((sqq, kq2), (sqk, kk2))):
                    for j in range(4):
                        a = 16 * (4 * n + j)
                        k = mm(pb[:, a:a + 16], s[:, 128 * j:128 * j + 128], kc[:, KC["heads"]], w, free)
                nm, y, t = (sq[:, 0, 128 * n:128 * n + 128] for n in range(3))
                yield c, dv, [k]
                k = ts(nm, pb[:, 0:128], 1e-24, None, ALU.max, None, k)
                ringA.free(i, k)
                yield c, dv, [k]
                k = yield from rsqrt(c, nm, y, t, k)
                wide = m2[:, :, :].rearrange("p a b -> p (a b)")
                yield c, dv, [k]
                yb = y.unsqueeze(2).to_broadcast([P, 128, 8])
                k = dv(lambda e, yb=yb, wide=wide: e.tensor_copy(wide.rearrange("p (h d) -> p h d", d=8), yb), 1.2, k, st.get("wide_read"))
                out = []
                for n, (s, w, d) in enumerate(((q_s, kq, qn), (k_s, kk, kw))):
                    yield c, pe, [ringA, k]
                    i, pb, free = ringA.take()
                    for j in range(4):
                        a = 128 * (4 * n + j)
                        k2 = tr(pb[:, 128 * j:128 * j + 128], wide[:, a:a + 128], k, free)
                    st["wide_read"] = k2
                    yield c, dv, [k2]
                    out.append(tt(dv, d, s, pb[:, :], ALU.mult, k2, w, done))
                    ringA.free(i, out[-1])
                yield c, dv, [out[1], kw_]
                kn = stt(kw, tw, 1.0, kw, ALU.add, ALU.mult, kw_, out[1])
                yield c, pe, [ringA]
                ia, acc, acc_free = ringA.take()
                ahead = None
                for r in range(9):
                    nxt = None
                    if r < 8:
                        yield c, pe, [ringA]
                        i, pb, free = ringA.take()
                        v0 = 128 * r
                        k = mm(pb[:, :], wb["wv"][:, v0:v0 + 128], x, free, ready)
                        pr = m1[:, r % 2, :]
                        yield c, dv, [k]
                        b1 = BA["bv"].start + r
                        k = stt(pr, pb[:, :], ba[:, b1:b1 + 1], kw, ALU.add, ALU.mult, k, kn)
                        ringA.free(i, k)
                        yield c, dv, [k]
                        k = red(Ar[:, r % 2, :], pr.rearrange("p (s t) -> p t s", s=NB), ALU.add, k, st.get(("Ar", r % 2)))
                        z = zr[r % 2]
                        yield c, po, [k]
                        k = tt(po, bt(z), bt(qn), Ar[:, r % 2, :].unsqueeze(1).to_broadcast([P, NB, W]), ALU.mult, k, out[0],
                               st.get(("zr", r % 2)), st.get(("x", c - 1)))
                        st["Ar", r % 2] = k
                        nxt = (r, z, k)
                    if ahead is not None:
                        r0, z0_, k0 = ahead
                        yield c, pe, [k0]
                        p0 = 128 * r0
                        ka = mm(acc[:, :], wb["perm"][:, p0:p0 + 128], z0_, k0, acc_free, st=(r0 == 0), sp_=(r0 == 7))
                        st["zr", r0 % 2] = ka
                    ahead = nxt
                yield c, dv, [ka, kr_]
                k = stt(tq, tq, 1.0, acc[:, :], ALU.add, ALU.mult, ka, kr_)
                ringA.free(ia, k)
                yield c, pe, [ringA, k]
                i, pb, free = ringA.take()
                k = mm(pb[:, :], wb["wo"], tq, free, k)
                st["fw_done"] = k
                yield c, dv, [k]
                k = stt(rC, pb[:, :], ba[:, BA["bo"]], x, ALU.add, ALU.add, k, ready, st.get(("x", c - 1)))
                ringA.free(i, k)
                st["x2_read", c] = k
                last = lambda xc, rstd, w: tt(dv, Xr[:, c, :], xc, rstd, ALU.mult, w)
                k = st["x", c] = yield from layernorm(c, ringA, 2, rC, k, last, st.get(("x", c - 1)))
                dma(g_keep, keep_d[:, c, :], Xr[:, c, :], k)

        L, where = {}, {}

        def lane_weights(layers):
            for l in layers:
                rank = 4 * NC * l - 3.5 if l else NC
                for n in range(6):
                    cols, raw = slice(512 * n, 512 * n + 512), stage[:, n % 2, :]
                    yield rank, sp, [L.get(("stage", n % 2))]
                    k = dma(g_big[n % 2], raw, wqkv_d[l, :, cols], L.get(("stage", n % 2)))
                    yield rank, ac, [k, K(l, "qkv_read", l - 1, n)]
                    k1 = act(wqkv[:, 0, cols], raw, ACT.Copy, k, L.get(("qkv_read", l - 1, n)))
                    yield rank, dv, [k1]
                    k2 = tt(dv, wqkv[:, 1, cols], raw, wqkv[:, 0, cols], ALU.subtract, k, k1, L.get(("qkv_read", l - 1, n)))
                    L["stage", n % 2] = [k1, k2]
                    L["wqkv", l, n] = [k1, k2]

        take_turns([recurrence(), ranked("A1", first_norm()), ranked("Ar", router()), ranked("As", shared()), ranked("Ae", experts()),
                    ranked("Af", fast_weights()), lane_weights([0])], st, RANK["soonA"])

        phase = [Tok(q, len(q.ops) - 1, q.clock) for q in (pe, dv, ac, po)]
        t_keep = Tok(g_keep, g_keep.n, sp.clock + 2.0)

        kT = big0[:, :].rearrange("p (r b s t) -> p r b s t", r=8, b=NB, s=2)
        V2 = big1[:, :].rearrange("p (b n) -> p b n", b=NB)
        z0 = po(lambda e: e.memset(big0[:, :], 0.0), 7.0, phase)
        z1 = po(lambda e: e.memset(big1[:, :], 0.0), 7.0, phase)
        rg = Ring(bank, [0, 1, 2, 3])
        for b in rg.readers:
            rg.readers[b] = phase
        units = [(l, c) for l in range(DEPTH) for c in range(NC)]
        tiles = [(u, i) for u in range(len(units)) for i in range(4)]
        NG, NU = len(tiles), len(units)
        t_vec = dma(g_vec, vec[:, :, :], vec_d)
        for c in range(NC):
            L["X", -1, c] = st["x", c]

        def load_rest(l):
            L["wo", l] = dma(g_wo, wo[:, :, :], wo_d[l], L.get(("wo_read", l - 1)), phase)

        def load_ffn(l):
            w = [L.get(("ffn_read", l - 1)), phase]
            dma(g_ffn, w1[:, :], w1_d[l], w)
            L["ffn", l] = dma(g_ffn, w2[:, :, :], w2_d[l], w)

        def shifted(rank, dst, c, kind, *after):
            v = Xr[:, c, :].rearrange("p (b t) -> p b t", b=NB)
            d = dst.rearrange("p (b t) -> p b t", b=NB)
            edge = zero if c == 0 else halo[:, kind, :]
            yield rank, ac, list(flat(after))
            a = [act(dst[0:64, :], Xr[0:64, c, :], ACT.Copy, *after)]
            yield rank, ac, []
            a.append(act(d[64:128, :, 1:W], v[64:128, :, 0:W - 1], ACT.Copy, *after))
            yield rank, ac, []
            a.append(act(d[64:128, :, 0], edge[64:128, :], ACT.Copy, *after, L.get(("halo", kind)), t_zero))
            yield rank, ac, [a[-1]]
            L["halo", kind] = act(halo[64:128, kind, :], v[64:128, :, W - 1], ACT.Copy, *after, a[-1])
            return a + [L["halo", kind]]

        def lane_x():
            for u, (l, c) in enumerate(units):
                rank = 4 * u + RANK["x"]
                hi, lo = xs[:, u % 2, 0, :], xs[:, u % 2, 1, :]
                wide = lambda ap: ap.rearrange("p (b t) -> p b t", b=NB)
                v = wide(Xr[:, c, :])
                edge = zero if c == 0 else halo[:, 0, :]
                yield rank, ac, [("X", l - 1, c), K(u >= 2, "xs_read", u - 2)]
                after = [L.get(("xs_read", u - 2)), L["X", l - 1, c], phase, L.get(("halo", 0)), t_zero]
                parts = [(hi[0:64, :], lo[0:64, :], Xr[0:64, c, :]),
                         (wide(hi)[64:128, :, 1:W], wide(lo)[64:128, :, 1:W], v[64:128, :, 0:W - 1]),
                         (wide(hi)[64:128, :, 0], wide(lo)[64:128, :, 0], edge[64:128, :])]
                ks = []
                for h, d, src in parts:
                    yield rank, ac, after
                    k = act(h, src, ACT.Copy, after)
                    yield rank, dv, [k]
                    ks += [k, tt(dv, d, src, h, ALU.subtract, k, after)]
                yield rank, ac, [ks[-1]]
                L["halo", 0] = act(halo[64:128, 0, :], v[64:128, :, W - 1], ACT.Copy, ks)
                L["xs", u] = ks + [L["halo", 0]]

        def lane_tables():
            kq = None
            for u, (l, c) in enumerate(units):
                rank = 4 * u - 4
                if c == 0:
                    yield rank, sp, []
                    kq = dma(g_qs[l % 2], qsb[:, l % 2, :, :], qs_d[l], L.get(("tab", u - 1)), phase)
                yield rank, sp, [K(u >= 2, "tab_read", u - 2, h) for h in range(2)]
                k = dma(g_tab[u % 2], tab[:, u % 2, :, :], tab_d[c], L.get(("tab_read", u - 2, 0)), L.get(("tab_read", u - 2, 1)), phase)
                yield rank, po, [k, kq]
                L["tab", u] = tt(po, tab[:, u % 2, :, :], tab[:, u % 2, :, :], qsb[:, l % 2, :, :], ALU.mult, k, kq)

        def lane_a():
            load_rest(0)
            load_ffn(0)
            for g, (u, i) in enumerate(tiles):
                l, c = units[u]
                rank = g + RANK["a"]
                xt = [xs[:, u % 2, n, 128 * i:128 * i + 128] for n in range(2)]
                for part in range(6):
                    room = K(g, "m1", g - 1, part) if part < 4 else K(g, "vst", g - 1, part - 4)
                    yield rank, pe, [rg, ("xs", u), ("wqkv", l, part), room]
                    ib, pb, free = rg.take()
                    col = 512 * part
                    k = mm3(pb[:, :], xt, [wqkv[:, n, col:col + 512] for n in range(2)], free, L["xs", u], L["wqkv", l, part])
                    L["proj", g, part] = k
                    where[g, part] = ib, pb
                    if i == 3 and c == NC - 1:
                        L["qkv_read", l, part] = k
                if i == 3:
                    L["xs_read", u] = k

        def lane_rotate(half):
            for g, (u, i) in enumerate(tiles):
                rank = g + RANK["a"]
                for part in range(half, 4, 2):
                    isk, s3 = part // 2, part % 2
                    yield rank, ac, [("proj", g, part)]
                    (ib, pb), k = where[g, part], L["proj", g, part]
                    ct, sn = tab[:, u % 2, 2 * isk, :], tab[:, u % 2, 2 * isk + 1, :]
                    o1 = m1[:, part, :].rearrange("p (h d) -> p h d", d=DH)
                    o2 = m2[:, s3, :].rearrange("p (h d) -> p h d", d=DH)
                    pv = pb[:, :].rearrange("p (h d) -> p h d", d=DH)
                    yield rank, ac, [k, L.get(("sq", s3))]
                    ks = act(sq[:, s3, :], pb[:, :], ACT.Square, k, L.get(("sq", s3)))
                    yield rank, dv, [ks, ("tab", u), K(g, "m1", g - 1, part)]
                    k1 = tt(dv, o1, pv, ct.unsqueeze(1).to_broadcast([P, 8, DH]), ALU.mult, k, ks, L["tab", u],
                            L.get(("m1", g - 1, part)))
                    yield rank, dv, [L.get(("m2", s3))]
                    k2 = tt(dv, o2[:, :, 0:32], pv[:, :, 32:64], sn[:, 0:32].unsqueeze(1).to_broadcast([P, 8, 32]), ALU.mult,
                            L.get(("m2", s3)))
                    k2 = tt(dv, o2[:, :, 32:64], pv[:, :, 0:32], sn[:, 32:64].unsqueeze(1).to_broadcast([P, 8, 32]), ALU.mult)
                    rg.free(ib, ks, k2)
                    if i == 3 and part >= 2:
                        L["tab_read", u, half] = k2
                    yield rank, dv, []
                    kr = red(ss[:, g % 2, 8 * part:8 * part + 8], sq[:, s3, :].rearrange("p (h d) -> p h d", d=DH), ALU.add, ks,
                             L.get(("ss", g - 2)))
                    L["sq", s3] = kr
                    yield rank, po, [k2]
                    ka = tt(po, m1[:, part, :], m1[:, part, :], m2[:, s3, :], ALU.add, k1, k2)
                    L["m2", s3] = ka
                    L["rotated", g, part] = (kr, ka)

        def lane_v():
            for g, (u, i) in enumerate(tiles):
                l, c = units[u]
                rank = g + RANK["v"]
                for par in range(2):
                    yield rank, ac, [("proj", g, 4 + par)]
                    (ib, pb), k = where[g, 4 + par], L["proj", g, 4 + par]
                    yield rank, ac, [k, K(g, "vst", g - 1, par)]
                    kv = act(vst[:, par, :], pb[:, :], ACT.Copy, k, L.get(("vst", g - 1, par)))
                    rg.free(ib, kv)
                    rows = 64 * par + 32 * (c % 2)
                    yield rank, sp, [kv, K(g >= 4, "av", g - 4)]
                    for b in range(4):
                        kd = dma(g_v[g % 4], V2[rows:rows + 32, 4 * i + b, :], vst[32 * b:32 * b + 32, par, :], kv, z1,
                                 L.get(("av", g - 4)))
                L["vst", g, 0] = L["vst", g, 1] = L["v", g] = kd

        def lane_n():
            for g in range(NG):
                rank = g + RANK["n"]
                yield rank, dv, [("rotated", g, part) for part in range(4)]
                kr, prods = zip(*(L["rotated", g, part] for part in range(4)))
                yield rank, dv, [*kr, K(g >= 2, "rot", g - 2)]
                nm, y, t = (nw[:, g % 2, n, 0:32] for n in range(3))
                k = ts(nm, ss[:, g % 2, :], 1e-24, None, ALU.max, None, kr, L.get(("nw", g % 2)))
                L["ss", g] = k
                yield rank, dv, [k]
                k = yield from rsqrt(rank, nm, y, t, k)
                ready = []
                for part, ka in enumerate(prods):
                    o1 = m1[:, part, :].rearrange("p (h d) -> p h d", d=DH)
                    rb = y[:, 8 * part:8 * part + 8].unsqueeze(2).to_broadcast([P, 8, DH])
                    yield rank, po, [k, ka]
                    ready.append(tt(po, o1, o1, rb, ALU.mult, k, ka))
                    L["rot", g, part] = ready[-1]
                L["nw", g % 2] = ready[-1]
                L["rot", g] = ready

        def lane_b(isk):
            for g, (u, i) in enumerate(tiles):
                l, c = units[u]
                rank = g + RANK["b"]
                done = []
                for h8 in range(2):
                    part = 2 * isk + h8
                    yield rank, pe, [rg, ("rot", g, part)]
                    ib, pb, free = rg.take()
                    for j in range(4):
                        k = tr(pb[:, 128 * j:128 * j + 128], m1[:, part, 128 * j:128 * j + 128], free, L["rot", g, part])
                    L["m1", g, part] = k
                    if isk:
                        d = kT[:, 4 * h8:4 * h8 + 4, 4 * i:4 * i + 4, c % 2, :]
                        yield rank, ac, [k, z0, K(g >= 4, "sim", g - 4)]
                        for j in range(4):
                            a = act(d[:, j], pb[:, 128 * j:128 * j + 128].rearrange("p (b t) -> p b t", b=4), ACT.Copy, k, z0,
                                    L.get(("sim", g - 4)))
                    else:
                        yield rank, ac, [k, K(g >= 2, "sim", g - 2)]
                        a = act(qT[:, g % 2, 4 * h8:4 * h8 + 4, :], pb[:, :].rearrange("p (r t) -> p r t", r=4), ACT.Copy, k,
                                L.get(("sim", g - 2)))
                    rg.free(ib, a)
                    done.append(a)
                L["T", g, isk] = done

        def lane_c():
            for g, (u, i) in enumerate(tiles):
                l, c = units[u]
                rank = g + RANK["c"]
                msk = kc[:, KC["mask"]].rearrange("p (v k) -> p v k", v=3)[:, 0 if c == 0 else 1 + c % 2, :]
                s = g % 2
                Sv = S[:, s, :].rearrange("p (r q k) -> p q r k", q=2, r=8)
                S16 = S[:, s, :].rearrange("p (h k) -> p h k", h=16)
                yield rank, pe, [("T", g, 0), ("T", g, 1), K(g, "masked", g - 1)]
                for r in range(8):
                    for par in range(2):
                        rows = slice(64 * par, 64 * par + 64)
                        for b in range(4):
                            k = mm(bank[4 + par][32 * b:32 * b + 32, 64 * r:64 * r + 64], qT[rows, s, r, 32 * b:32 * b + 32],
                                   kT[rows, r, 4 * i + b, :, :].rearrange("p s t -> p (s t)"), L["T", g, 0], L["T", g, 1],
                                   L.get(("masked", g - 1)), z0)
                L["sim", g] = k
                ka = []
                for par in range(2):
                    pv = bank[4 + par][:, :].rearrange("p (r k) -> p r k", r=8)
                    yield rank, dv, [k, K(g >= 2, "S", g - 2)]
                    ka.append(tt(dv, Sv[:, par], pv, msk.unsqueeze(1).to_broadcast([P, 8, 64]), ALU.add, k,
                                 L.get(("S", g - 2)), phase))
                L["masked", g] = ka

        def lane_s():
            for g in range(NG):
                rank = g + RANK["c"]
                s = g % 2
                S16 = S[:, s, :].rearrange("p (h k) -> p h k", h=16)
                yield rank, dv, [("masked", g)]
                k = red(mx[:, s, 0, :], S16, ALU.max, L["masked", g])
                yield rank, po, [k]
                k = tt(po, S16, S16, mx[:, s, 0, :].unsqueeze(2).to_broadcast([P, 16, 64]), ALU.subtract, k)
                yield rank, ac, [k]
                kx = act(S[:, s, :], S[:, s, :], ACT.Exp, k)
                L["exp", g] = kx
                yield rank, dv, [kx]
                k = red(mx[:, s, 1, :], S16, ALU.add, kx)
                L["summed", g] = k
                yield rank, dv, [k]
                L["sum", g] = dv(lambda e, s=s: e.reciprocal(rs[:, s, 0, :], mx[:, s, 1, :]), 0.2, k, L.get(("On", g - 2)))

        def lane_p():
            for g in range(NG):
                rank = g + RANK["p"]
                ko = []
                for h in range(2):
                    yield rank, pe, [rg, ("exp", g)]
                    ib, pb, free = rg.take()
                    for j in range(4):
                        r = 4 * h + j
                        k = tr(pb[:, 128 * j:128 * j + 128], S[:, g % 2, 128 * r:128 * r + 128], free, L["exp", g])
                    yield rank, ac, [k, K(g, "av", g - 1)]
                    ko.append(act(P2[:, 4 * h:4 * h + 4, :], pb[:, :].rearrange("p (r t) -> p r t", r=4), ACT.Copy, k,
                                  L.get(("av", g - 1))))
                    rg.free(ib, ko[-1])
                yield rank, dv, [("summed", g)]
                L["S", g] = [k, L["summed", g]]
                L["P2", g] = ko

        def lane_d():
            for g, (u, i) in enumerate(tiles):
                s = g % 2
                ko = []
                yield g, pe, [("P2", g), ("v", g), K(g, "On", g - 1)]
                for r in range(8):
                    for par in range(2):
                        rows = slice(64 * par, 64 * par + 64)
                        for b in range(4):
                            k = mm(bank[6 + par][32 * b:32 * b + 32, 64 * r:64 * r + 64], P2[rows, r, 32 * b:32 * b + 32],
                                   V2[rows, 4 * i + b, 64 * r:64 * r + 64], L["P2", g], L["v", g], L.get(("On", g - 1)), z1)
                L["av", g] = k
                for par in range(2):
                    yield g, dv, [k, ("sum", g), K(g, "OnT", g - 1)]
                    o = On[:, 0, :].rearrange("p (r q d) -> p r q d", q=2, d=DH)[:, :, par, :]
                    rb = rs[:, s, 0, :].rearrange("p (r q) -> p q r", q=2)[:, par].unsqueeze(2).to_broadcast([P, 8, DH])
                    ko.append(tt(dv, o, bank[6 + par][:, :].rearrange("p (r d) -> p r d", d=DH), rb, ALU.mult, k, L["sum", g],
                                 L.get(("OnT", g - 1))))
                L["On", g] = ko

        def lane_e():
            for g in range(NG):
                ko = []
                rank = g + RANK["e"]
                for h8 in range(2):
                    yield rank, pe, [rg, ("On", g)]
                    ib, pb, free = rg.take()
                    for j in range(4):
                        r = 4 * h8 + j
                        k = tr(pb[:, 128 * j:128 * j + 128], On[:, 0, 128 * r:128 * r + 128], free, L["On", g])
                    yield rank, ac, [k, K(g >= 2, "OT_read", g - 2)]
                    a = act(OT[:, g % 2, 4 * h8:4 * h8 + 4, :], pb[:, :].rearrange("p (r t) -> p r t", r=4), ACT.Copy, k,
                            L.get(("OT_read", g - 2)))
                    rg.free(ib, a)
                    ko.append(a)
                L["OnT", g] = k
                L["OT", g] = ko

        def lane_w():
            for g, (u, i) in enumerate(tiles):
                l, c = units[u]
                rank = g + RANK["w"]
                yield rank, pe, [rg, ("OT", g), ("wo", l)]
                ib, pb, free = rg.take()
                for r in range(8):
                    k = mm(pb[:, 0:128], wo[:, r, :], OT[:, g % 2, r, :], free, L["OT", g], L["wo", l], st=(r == 0),
                           sp_=(r == 7))
                L["OT_read", g] = k
                L["wo_read", l] = k
                if i == 3 and c == NC - 1 and l + 1 < DEPTH:
                    load_rest(l + 1)
                xv = Xr[:, c, 128 * i:128 * i + 128]
                yield rank, dv, [k]
                k = tt(dv, xv, pb[:, 0:128], xv, ALU.add, k, L["xs", u], L["X", l - 1, c])
                rg.free(ib, k)
                L["res", g] = k

        def lane_f():
            for u, (l, c) in enumerate(units):
                rank = 4 * u + RANK["f"]
                v = lambda n, rows=P, l=l: vec[0:rows, l, n:n + 1]
                yield rank, ac, [("res", 4 * u + i) for i in range(4)]
                ready = [L["res", 4 * u + i] for i in range(4)]
                a = yield from shifted(rank, x2s[:, :], c, 1, ready, L.get("x2s_read"))

                def last(xc, rstd, w):
                    return tt(dv, xn[:, :], xc, rstd, ALU.mult, w, L.get("xn_read"))

                k = yield from layernorm(rank, rg, 0, x2s[:, :], a, last, L.get("ln"))
                L["x2s_read"] = L["ln"] = k
                yield rank, ac, [k]
                kn = act(xn[:, :], xn[:, :], ACT.Identity, k, t_vec, scale=v(7), bias=v(8))
                kgs = []
                for f, rows in enumerate(FB):
                    yield rank + RANK["f1"], pe, [rg, kn, ("ffn", l)]
                    ig, pg, free = rg.take()
                    kg = mm(pg[0:rows, :], w1[:, DI + 128 * f:DI + 128 * f + rows], xn[:, :], free, kn, L["ffn", l])
                    yield rank + RANK["f1"], ac, [kg]
                    kgs.append(act(gg[0:rows, f, :], pg[0:rows, :], ACT.Gelu, kg, L.get(("gg", f)), bias=v(3 + f, rows)))
                    rg.free(ig, kgs[-1])
                kh = []
                for f, rows in enumerate(FB):
                    yield rank + RANK["f1"], pe, [rg]
                    ia, pa, free = rg.take()
                    ka = mm(pa[0:rows, :], w1[:, 128 * f:128 * f + rows], xn[:, :], free)
                    yield rank + RANK["f1"], dv, [ka, kgs[f], L.get("hh_read")]
                    k = stt(hh[0:rows, f, :], pa[0:rows, :], v(f, rows), gg[0:rows, f, :], ALU.add, ALU.mult, ka, kgs[f],
                            L.get("hh_read"))
                    L["gg", f] = k
                    rg.free(ia, k)
                    kh.append(k)
                L["xn_read"] = ka
                yield rank + RANK["f2"], pe, [rg, *kh]
                ib, pb, free = rg.take()
                for f, rows in enumerate(FB):
                    k = mm(pb[:, :], w2[0:rows, f, :], hh[0:rows, f, :], free, kh, st=(f == 0), sp_=(f == 2))
                L["hh_read"] = L["ffn_read", l] = k
                if c == NC - 1 and l + 1 < DEPTH:
                    load_ffn(l + 1)
                yield rank + RANK["f2"], dv, [k]
                k = stt(Xr[:, c, :], pb[:, :], v(6), Xr[:, c, :], ALU.add, ALU.add, k, a, ready)
                rg.free(ib, k)
                L["X", l, c] = k
                if l == DEPTH - 1:
                    kd = dma(g_back[c % 2], back, keep_d[:, c, :], t_keep, L.get("back"), L["stage", 0])
                    yield rank + RANK["f2"], dv, [k, kd]
                    k = tt(dv, Xr[:, c, :], Xr[:, c, :], back, ALU.add, k, kd)
                    L["back"] = k
                    end = lambda xc, rstd, w, c=c: tt(dv, Xr[:, c, :], xc, rstd, ALU.mult, w)
                    k = yield from layernorm(rank + RANK["f2"], rg, 0, Xr[:, c, :], k, end, L["ln"])
                    L["ln"] = k
                    dma(g_out, out_d[:, c, :], Xr[:, c, :], k)

        take_turns([lane_weights(range(1, DEPTH)), lane_tables(), lane_d(), lane_p(), lane_s(), lane_c(), lane_b(0), lane_b(1), lane_n(), lane_rotate(0), lane_rotate(1), lane_v(), lane_a(), lane_x(), lane_e(), lane_w(), lane_f()], L, RANK["soon"])
        sp(lambda e: None, 0.0, Tok(g_out, g_out.n, 0.0), Tok(g_keep, g_keep.n, 0.0))

        value = count_up([pe, dv, ac, po, sp])
        block = ctx.enter_context(nc.Block())

        def play_dma(q, eng):
            seen = {}
            for fn, after in q.ops:
                for t in flat(after):
                    v = value[(t.q, t.at)] if isinstance(t.q, Queue) else t.at
                    if seen.get(t.q, 0) < v:
                        eng.wait_ge(t.q.sem, v)
                        seen[t.q] = v
                fn(eng)

        @block.sync
        def _(eng):
            play_dma(sp, eng)

        @block.tensor
        def _(eng):
            play(pe, eng, value)

        @block.vector
        def _(eng):
            play(dv, eng, value)

        @block.scalar
        def _(eng):
            play(ac, eng, value)

        @block.gpsimd
        def _(eng):
            play(po, eng, value)


def shape_constants():
    f = np.float32
    kc, perm = np.zeros((P, KC_N), f), np.zeros((P, 8 * P), f)
    kc[:, KC["ident"]] = np.eye(P, dtype=f)
    kc[:, KC["center"]] = np.eye(P, dtype=f) - f(1.0 / P)
    n = np.arange(P)
    for r in range(8):
        m = np.zeros((P, P), f)
        m[n, 8 * (n // 8) + (n % 8 + r) % 8] = 0.25
        perm[:, P * r:P * r + P] = m
    kc[n, KC["heads"].start + n // 8] = 1.0
    kc[:, KC["mean"]] = 1.0 / P
    kc[:, KC["rank"]] = np.arange(8, 0, -1)
    low = f(-np.finfo(f).max)
    a, b = (n % W)[:, None], np.arange(W)[None, :]
    cur, prev = np.where(b <= a, f(0), low), np.where(b >= a, f(0), low)
    none = np.full((P, W), low, f)
    kc[:, KC["mask"]] = np.concatenate([cur, none, cur, prev, prev, cur], 1)
    half = np.arange(0, DH, 2, dtype=f)
    inv = (f(1.0) / np.power(f(10000.0), half / f(DH))).astype(f)
    t = np.arange(NT, dtype=f)
    fr = t[:, None] * inv[None, :]
    fr = np.concatenate([fr, fr], -1).astype(np.float64)
    base = ((half + f(0.4 * DH)) / f(1.4 * DH)).astype(f)
    power = (t - f(NT // 2)) / f(W // 2)
    sc = np.power(base[None, :].astype(np.float64), power[:, None].astype(np.float64))
    sc = np.concatenate([sc, sc], -1)
    sign = np.concatenate([-np.ones(DH // 2), np.ones(DH // 2)])
    tabs = np.stack([8.0 * np.cos(fr) * sc, 8.0 * np.sin(fr) * sc * sign, np.cos(fr) / sc, np.sin(fr) / sc * sign])
    tabs = tabs.reshape(4, NC, W, DH).transpose(2, 0, 1, 3)
    return kc, perm, np.tile(tabs, (4, 1, 1, 1)).astype(f)


def kernel(**inputs):
    import concourse.bacc as bacc
    from concourse.bass_utils import run_bass_kernel_spmd

    a = {k: np.asarray(v) for k, v in inputs.items()}
    f = np.float32
    kc, perm, tabs = shape_constants()
    rot = lambda w, r: np.concatenate([np.roll(w[8 * h:8 * h + 8], -r, 0) for h in range(16)])
    A = lambda n: a["L1_attn_" + n]
    down = lambda w: w.T.reshape(2, 128, 128).transpose(1, 0, 2).reshape(128, 256)
    wa = np.zeros((P, WA_N), f)
    put = {"ws": a["L0_attn_W_state"].T, "wg": a["L0_attn_W_gate"].T, "router": a["L0_ffn_gate_w"].T,
           "sg": a["L0_ffn_shared_gate"].T, "su": a["L0_ffn_shared_up"].T, "sd": down(a["L0_ffn_shared_down"]),
           "eg": a["L0_ffn_r_gate"].transpose(2, 0, 1).reshape(128, -1),
           "eu": a["L0_ffn_r_up"].transpose(2, 0, 1).reshape(128, -1),
           "ed": np.concatenate([down(w) for w in a["L0_ffn_r_down"]], 1),
           "wq": A("Wq_w").T, "wk": A("Wk_w").T, "ww": np.repeat(A("Ww_w").T, 8, 1), "wr": np.repeat(A("Wr_w").T, 8, 1),
           "wv": np.concatenate([rot(A("Wv_w"), r).T for r in range(8)], 1), "wo": A("Wo_w").T}
    wb = np.zeros((P, WB_N), f)
    put["perm"] = perm
    for n, w in put.items():
        if n in WA:
            wa[:, WA[n]] = w
        else:
            wb[:, WB[n]] = w
    ba = np.zeros((P, BA_N), f)
    put = {"bs": a["L0_attn_b_state"][:, None], "bg": a["L0_attn_b_gate"][:, None], "bq": A("Wq_b")[:, None],
           "bk": A("Wk_b")[:, None], "bw": np.repeat(A("Ww_b"), 8)[:, None], "br": np.repeat(A("Wr_b"), 8)[:, None],
           "bv": np.stack([rot(A("Wv_b"), r) for r in range(8)], 1), "bo": A("Wo_b")[:, None]}
    for n, w in put.items():
        ba[:, BA[n]] = w
    B = lambda n: a["L1_ffn_" + n]
    swap = lambda s: np.concatenate([s[:, 32:], s[:, :32]], 1)
    qs = np.stack([B("q_scale"), swap(B("q_scale")), B("k_scale"), swap(B("k_scale"))], 1)
    qs = np.ascontiguousarray(np.broadcast_to(qs[:, None], (DEPTH, P, 4, DH)))
    wv = B("Wqkv")[:, :, 2 * INNER:].reshape(DEPTH, C, 8, 2, DH).transpose(0, 1, 3, 2, 4).reshape(DEPTH, C, INNER)
    wqkv = np.concatenate([B("Wqkv")[:, :, :2 * INNER], wv], 2)
    w2 = np.zeros((DEPTH, 3 * P, C), f)
    w2[:, :DI] = B("W2")
    vec = np.zeros((P, DEPTH, 9), f)
    for l in range(DEPTH):
        for n in range(2):
            for m, rows in enumerate(FB):
                vec[:rows, l, 3 * n + m] = B("b1")[l, DI * n + 128 * m:DI * n + 128 * m + rows]
        vec[:, l, 6], vec[:, l, 7], vec[:, l, 8] = B("b2")[l], B("ln_g")[l], B("ln_b")[l]
    arrays = {
        "x": a["L0_attn_x"].reshape(NB, NC, W, C).transpose(3, 1, 0, 2).reshape(C, NC, N),
        "kc": kc, "wa": wa, "wb": wb, "ba": ba, "tab": tabs.transpose(2, 0, 1, 3), "qs": qs, "wqkv": wqkv,
        "wo": B("Wo").reshape(DEPTH, 8, 128, C).transpose(0, 2, 1, 3), "w1": B("W1"),
        "w2": w2.reshape(DEPTH, 3, P, C).transpose(0, 2, 1, 3), "vec": vec,
    }
    nc = bacc.Bacc("TRN2", target_bir_lowering=False, num_devices=1)
    ins, args = {}, []
    for n, v in arrays.items():
        v = np.ascontiguousarray(v)
        ins["in_" + n] = v
        args.append(nc.dram_tensor("in_" + n, v.shape, F32, kind="ExternalInput").ap())
    out = nc.dram_tensor("out", (C, NC, N), F32, kind="ExternalOutput").ap()
    keep = nc.dram_tensor("keep", (C, NC, N), F32, kind="Internal").ap()
    program(nc, *args, out, keep)
    r = run_bass_kernel_spmd(nc, [ins], core_ids=[0])
    y = np.asarray(r.results[0]["out"])
    return np.ascontiguousarray(y.reshape(C, NC, NB, W).transpose(2, 1, 3, 0)).reshape(NB, NT, C)
```
